# Optimizing a Trainium2 kernel written in Bass

```python
import numpy as np
import jax
import jax.numpy as jnp

def _softmax(x, axis=-1):
    return jax.nn.softmax(x, axis=axis)

def _gelu(x):
    return jax.nn.gelu(x, approximate=True)

def _silu(x):
    return jax.nn.silu(x)

def _sigmoid(x):
    return jax.nn.sigmoid(x)

def _layernorm(x, axis=-1, eps=1e-05):
    m = jnp.mean(x, axis=axis, keepdims=True)
    v = jnp.var(x, axis=axis, keepdims=True)
    return (x - m) / jnp.sqrt(v + eps)

def _scatter_add(tgt, idx, src, axis=0):
    return tgt.at[idx].add(src)

def _segment_sum(src, seg, n):
    return jax.ops.segment_sum(src, seg, n)
kernel_name = 'mk_adj_resnorm_d1_adj_r2_a54746'

def setup_inputs(seed: int=0):
    np.random.seed(seed)
    _w = jnp.asarray

    def _rec_inputs():
        import jax
        import jax.numpy as jnp
        _gk = jax.random.key(seed)
        x = -0.001547 + 1.001 * jax.random.normal(jax.random.fold_in(_gk, 1), (64, 128, 128), jnp.float32)
        _w = (1.0 + jnp.arange(128, dtype=jnp.float32)) ** (-0.5)
        _w = _w / _w.mean()
        _pij = jnp.clip(0.015625 * _w[:, None] * _w[None, :], 0.0, 1.0)
        _a = jax.random.uniform(jax.random.fold_in(_gk, 2), (64, 128, 128)) < _pij
        _a = jnp.logical_or(_a, jnp.eye(128, dtype=bool))
        adj = _a.astype(jnp.int32)
        _nm = jnp.ones((64, 128), dtype=bool)
        nodemask = jnp.where(_nm, 1.0, 0.0).astype(jnp.float32)
        return (x, adj, nodemask)
    x, adj, nodemask = _rec_inputs()

    def _L0_gnn_setup():
        import jax, jax.numpy as jnp
        import numpy as np
        D_MODEL = 128
        NUM_REL = 40

        def _direction(x, W, Wg, b, bg, adj, rel_ids):
            h = x @ W.T
            g = h @ Wg.T
            vals = (h[:, :, None, :] + b) * jax.nn.sigmoid(g[:, :, None, :] + bg)
            onehot = (adj[..., None] == rel_ids).astype(h.dtype)
            return jnp.einsum('bnmr,bmrd->bnd', onehot, vals)
        key = jax.random.key(seed)
        ks = jax.random.split(key, 16)
        B, N, d = (2, 256, D_MODEL)
        s = 0.02
        inp = {'node': jax.random.normal(ks[0], (B, N, d), dtype=jnp.float32), 'node_mask': jnp.ones((B, N), dtype=jnp.float32), 'adj_mat': jax.random.randint(ks[1], (B, N, N), 0, 41, dtype=jnp.int32), 'W_fwd': jax.random.normal(ks[2], (d, d), dtype=jnp.float32) * s, 'W_bwd': jax.random.normal(ks[3], (d, d), dtype=jnp.float32) * s, 'W_loop': jax.random.normal(ks[4], (d, d), dtype=jnp.float32) * s, 'Wg_fwd': jax.random.normal(ks[5], (d, d), dtype=jnp.float32) * s, 'Wg_bwd': jax.random.normal(ks[6], (d, d), dtype=jnp.float32) * s, 'Wg_loop': jax.random.normal(ks[7], (d, d), dtype=jnp.float32) * s, 'b_fwd': jax.random.normal(ks[8], (NUM_REL - 1, d), dtype=jnp.float32) * s, 'b_bwd': jax.random.normal(ks[9], (NUM_REL - 1, d), dtype=jnp.float32) * s, 'b_loop': jax.random.normal(ks[10], (1, d), dtype=jnp.float32) * s, 'bg_fwd': jax.random.normal(ks[11], (NUM_REL - 1, d), dtype=jnp.float32) * s, 'bg_bwd': jax.random.normal(ks[12], (NUM_REL - 1, d), dtype=jnp.float32) * s, 'bg_loop': jax.random.normal(ks[13], (1, d), dtype=jnp.float32) * s}
        return inp
    _L0_gnn_all = _L0_gnn_setup()
    _L0_gnn_in = {k: v for k, v in _L0_gnn_all.items() if k in ('W_fwd', 'W_bwd', 'W_loop', 'Wg_fwd', 'Wg_bwd', 'Wg_loop', 'b_fwd', 'b_bwd', 'b_loop', 'bg_fwd', 'bg_bwd', 'bg_loop')}
    del _L0_gnn_all
    return {'x': x, 'adj': adj, 'nodemask': nodemask, 'L0_gnn_W_fwd': _L0_gnn_in['W_fwd'], 'L0_gnn_W_bwd': _L0_gnn_in['W_bwd'], 'L0_gnn_W_loop': _L0_gnn_in['W_loop'], 'L0_gnn_Wg_fwd': _L0_gnn_in['Wg_fwd'], 'L0_gnn_Wg_bwd': _L0_gnn_in['Wg_bwd'], 'L0_gnn_Wg_loop': _L0_gnn_in['Wg_loop'], 'L0_gnn_b_fwd': _L0_gnn_in['b_fwd'], 'L0_gnn_b_bwd': _L0_gnn_in['b_bwd'], 'L0_gnn_b_loop': _L0_gnn_in['b_loop'], 'L0_gnn_bg_fwd': _L0_gnn_in['bg_fwd'], 'L0_gnn_bg_bwd': _L0_gnn_in['bg_bwd'], 'L0_gnn_bg_loop': _L0_gnn_in['bg_loop']}

def reference(x, adj, nodemask, L0_gnn_W_fwd, L0_gnn_W_bwd, L0_gnn_W_loop, L0_gnn_Wg_fwd, L0_gnn_Wg_bwd, L0_gnn_Wg_loop, L0_gnn_b_fwd, L0_gnn_b_bwd, L0_gnn_b_loop, L0_gnn_bg_fwd, L0_gnn_bg_bwd, L0_gnn_bg_loop):
    import jax
    import jax.numpy as jnp

    def _L0_gnn_ref(node, node_mask, adj_mat, W_fwd, W_bwd, W_loop, Wg_fwd, Wg_bwd, Wg_loop, b_fwd, b_bwd, b_loop, bg_fwd, bg_bwd, bg_loop):
        import jax, jax.numpy as jnp
        import numpy as np
        D_MODEL = 128
        NUM_REL = 40

        def _direction(x, W, Wg, b, bg, adj, rel_ids):
            h = x @ W.T
            g = h @ Wg.T
            vals = (h[:, :, None, :] + b) * jax.nn.sigmoid(g[:, :, None, :] + bg)
            onehot = (adj[..., None] == rel_ids).astype(h.dtype)
            return jnp.einsum('bnmr,bmrd->bnd', onehot, vals)
        rels = jnp.arange(2, NUM_REL + 1, dtype=adj_mat.dtype)
        rel1 = jnp.array([1], dtype=adj_mat.dtype)
        adj_t = jnp.swapaxes(adj_mat, -1, -2)
        out = _direction(node, W_fwd, Wg_fwd, b_fwd, bg_fwd, adj_mat, rels)
        out = out + _direction(node, W_bwd, Wg_bwd, b_bwd, bg_bwd, adj_t, rels)
        out = out + _direction(node, W_loop, Wg_loop, b_loop, bg_loop, adj_t, rel1)
        return jax.nn.relu(out)
    x = _layernorm(x + _L0_gnn_ref(x, nodemask, adj, L0_gnn_W_fwd, L0_gnn_W_bwd, L0_gnn_W_loop, L0_gnn_Wg_fwd, L0_gnn_Wg_bwd, L0_gnn_Wg_loop, L0_gnn_b_fwd, L0_gnn_b_bwd, L0_gnn_b_loop, L0_gnn_bg_fwd, L0_gnn_bg_bwd, L0_gnn_bg_loop), axis=-1)
    return x

_drawn_inputs = setup_inputs


def setup_inputs(seed=0):
    import zlib

    import numpy as np

    out = dict(_drawn_inputs(seed))
    spreads = {}
    factors = {'L0_gnn_Wg_loop': 8.0, 'L0_gnn_bg_loop': 41.459}
    for name, (base, spread) in spreads.items():
        noise = np.random.default_rng([zlib.crc32(name.encode()), seed]).standard_normal(out[name].shape)
        drawn = base * np.exp(spread * noise) if base else spread * noise
        out[name] = jnp.asarray(drawn.astype(out[name].dtype))
    for name, factor in factors.items():
        out[name] = (out[name] * factor).astype(out[name].dtype)
    return out
```

```python
from contextlib import ExitStack

import numpy as np

import concourse.bass as bass
from concourse import mybir

F32 = mybir.dt.float32
BF16 = mybir.dt.bfloat16
I32 = mybir.dt.int32
U32 = mybir.dt.uint32
ALU = mybir.AluOpType
ACT = mybir.ActivationFunctionType
AX = mybir.AxisListType

B = 64
N = 128
D = 128
R = 39
FIRST_REL = 2
EPS = 1e-5

GB = 4
GROUPS = B // GB
RING = 4
ROUNDS = GROUPS // RING
STORE_LAG = 7


def gnn_resnorm_kernel(nc, x, adj, w_fwd, w_bwd, w_loop, wg_fwd, wg_bwd, wg_loop,
                       b_fwd, b_bwd, b_loop, bg_fwd, bg_bwd, bg_loop, out):
    x_g = x.rearrange("(g b) n d -> g n b d", b=GB)
    adj_g = adj.rearrange("(g b) n m -> g n b m", b=GB)
    out_g = out.rearrange("(g b) n d -> g n b d", b=GB)

    ctx = ExitStack()
    with ctx:
        def sb(name, shape, dt):
            return ctx.enter_context(nc.sbuf_tensor(name, shape, dt))

        def sem(name):
            return ctx.enter_context(nc.semaphore(name))

        def ring_sem(name):
            return [sem(f"{name}{k}") for k in range(RING)]

        ident = sb("ident", [128, 128], F32)
        ones = sb("ones", [128, 128], BF16)
        minus_half = sb("minus_half", [128, GB], F32)
        w_nat = sb("w_nat", [128, 3, D], F32)
        wg_nat = sb("wg_nat", [128, 3, D], F32)
        wgT = sb("wgT", [128, 3, D], F32)
        wcat_loop = sb("wcat_loop", [128, 2, D], F32)
        bias_f = sb("bias_f", [128, 2, D], F32)
        bias_r = sb("bias_r", [128, 2, D], F32)
        bias_p = sb("bias_p", [128, 3, 2, D], BF16)
        bias_s = sb("bias_s", [128, 2, D], F32)
        bias_rows = sb("bias_rows", [128, 2, 2, D], BF16)

        x_sb = sb("x_sb", [128, RING, GB, D], F32)
        adj_sb = sb("adj_sb", [128, RING, GB, N], I32)
        mask = sb("mask", [128, RING, GB, N], F32)
        xT = sb("xT", [128, RING, GB * N], F32)
        gate = sb("gate", [128, 2, GB, D], F32)
        vals = sb("vals", [128, RING, GB, D], F32)
        y = sb("y", [128, RING, GB, D], F32)
        o_sb = sb("o_sb", [128, RING, GB, D], F32)
        bn = sb("bn", [128, RING, GB, 6], F32)
        mean_var = sb("mean_var", [128, RING, GB, 2], F32)
        var_eps = sb("var_eps", [128, RING, GB], F32)
        neg_mean = sb("neg_mean", [128, RING, GB], F32)
        rstd = sb("rstd", [128, RING, GB], F32)
        shift = sb("shift", [128, RING, GB], F32)

        excess = sb("excess", [128, RING, GB, N], BF16)
        row_excess = sb("row_excess", [128, GROUPS], F32)
        row_max = sb("row_max", [128, 1], F32)
        all_max = sb("all_max", [1, 1], F32)
        general = sb("general", [1, 1], I32)

        wcat_dir = sb("wcat_dir", [128, 4, D], F32)
        rel_b = sb("rel_b", [128, R, 2, D], F32)
        rel_bg = sb("rel_bg", [128, R, 2, D], F32)
        rel_id = sb("rel_id", [128, R], F32)
        gx = sb("gx", [128, D], F32)
        gadj = sb("gadj", [128, N], I32)
        gadj_pair = sb("gadj_pair", [128, 2, N], F32)
        gxT = sb("gxT", [128, N], F32)
        gh = sb("gh", [128, 4, D], F32)
        gh_b = sb("gh_b", [128, 2, D], F32)
        gg_b = sb("gg_b", [128, 2, D], F32)
        ggate = sb("ggate", [128, 2, D], F32)
        gvals = sb("gvals", [128, 2, D], F32)
        gmask = sb("gmask", [128, 2, N], F32)
        gy = sb("gy", [128, D], F32)
        gbn = sb("gbn", [128, 6], F32)
        gmv = sb("gmv", [128, 2], F32)
        gve = sb("gve", [128, 1], F32)
        grstd = sb("grstd", [128, 1], F32)
        go = sb("go", [128, D], F32)

        xT_ps = [ctx.enter_context(nc.psum_tensor(f"xT_ps{i}", [128, 512], F32)) for i in range(2)]
        hg_ps = [ctx.enter_context(nc.psum_tensor(f"hg_ps{i}", [128, GB, 2, D], F32)) for i in range(2)]
        sum_ps = [ctx.enter_context(nc.psum_tensor(f"sum_ps{i}", [128, GB, D], F32)) for i in range(2)]

        weights_in = sem("weights_in")
        bias_in = sem("bias_in")
        ident_cleared = sem("ident_cleared")
        ident_ready = sem("ident_ready")
        const_ready = sem("const_ready")
        wT_done = sem("wT_done")
        wT_copied = sem("wT_copied")
        wprod_done = sem("wprod_done")
        wcat_ready = sem("wcat_ready")
        bias_step = sem("bias_step")

        x_in = ring_sem("x_in")
        adj_in = ring_sem("adj_in")
        mask_ready = ring_sem("mask_ready")
        adj_tested = ring_sem("adj_tested")
        xT_done = ring_sem("xT_done")
        xT_ready = ring_sem("xT_ready")
        hg_done = ring_sem("hg_done")
        gate_ready = ring_sem("gate_ready")
        vals_ready = ring_sem("vals_ready")
        sums_done = ring_sem("sums_done")
        y_ready = ring_sem("y_ready")
        bn_done = ring_sem("bn_done")
        stats_ready = ring_sem("stats_ready")
        rstd_step = sem("rstd_step")
        shift_ready = ring_sem("shift_ready")
        o_ready = ring_sem("o_ready")
        stored = ring_sem("stored")

        waits_apart = sem("waits_apart")
        row_max_ready = sem("row_max_ready")
        row_max_T = sem("row_max_T")
        all_max_ready = sem("all_max_ready")
        general_ready = sem("general_ready")

        g_weights_in = sem("g_weights_in")
        g_rel_in = sem("g_rel_in")
        g_rel_id = sem("g_rel_id")
        g_wT_done = sem("g_wT_done")
        g_wT_copied = sem("g_wT_copied")
        g_wprod_done = sem("g_wprod_done")
        g_wcat_ready = sem("g_wcat_ready")
        g_in = sem("g_in")
        g_adj_f = sem("g_adj_f")
        g_T_done = sem("g_T_done")
        g_T_ready = sem("g_T_ready")
        g_h_done = sem("g_h_done")
        g_h_copied = sem("g_h_copied")
        g_loop_gate = sem("g_loop_gate")
        g_loop_vals = sem("g_loop_vals")
        g_loop_sum = sem("g_loop_sum")
        g_biased = sem("g_biased")
        g_h_biased = sem("g_h_biased")
        g_gate = sem("g_gate")
        g_vals = sem("g_vals")
        g_rel_sum = sem("g_rel_sum")
        g_stat = sem("g_stat")
        g_rstd = sem("g_rstd")
        g_o = sem("g_o")
        g_stored = sem("g_stored")

        def run_slots(eng, slot, lag, peeled=1):
            for s in range(peeled * RING):
                slot(s // RING, s % RING)
            with eng.Fori(peeled, ROUNDS) as rnd:
                for k in range(RING):
                    slot(rnd, k)
            for s in range(lag):
                slot(ROUNDS + s // RING, s % RING)

        def at(rnd, k, back):
            q = (k - back) // RING
            if isinstance(rnd, int) and not 0 <= rnd + q < ROUNDS:
                return None
            return (k - back) % RING, (rnd + q if q else rnd)

        def wait(eng, sems, group, unit=1):
            if group is not None:
                k, rnd = group
                eng.wait_ge(sems[k], (rnd + 1) * unit)

        def wait_apart(eng, one, value):
            eng.wait_ge(one, value)
            eng.sem_inc(waits_apart, 1)

        def wait_all_stored(eng):
            for k in range(RING):
                eng.wait_ge(stored[k], 16 * ROUNDS)

        block = ctx.enter_context(nc.Block())

        @block.sync
        def _(sp):
            sp.dma_start(w_nat[:, 0, :], w_loop).then_inc(weights_in, 16)
            sp.dma_start(wg_nat[:, 0, :], wg_loop).then_inc(weights_in, 16)
            sp.dma_start(bias_f[:, 0, :], b_loop.partition_broadcast(128)).then_inc(bias_in, 16)
            sp.dma_start(bias_f[:, 1, :], bg_loop.partition_broadcast(128)).then_inc(bias_in, 16)

            def slot(rnd, k):
                here = at(rnd, k, 0)
                if here is not None:
                    if at(rnd, k, RING) is not None:
                        wait_apart(sp, y_ready[k], rnd)
                    group = rnd * RING + k
                    sp.dma_start(x_sb[:, k, :, :], x_g[group]).then_inc(x_in[k], 16)
                    wait(sp, adj_tested, at(rnd, k, RING))
                    wait(sp, mask_ready, at(rnd, k, RING))
                    sp.dma_start(adj_sb[:, k, :, :], adj_g[group]).then_inc(adj_in[k], 16)
                back = at(rnd, k, STORE_LAG)
                if back is not None:
                    j = back[0]
                    wait_apart(sp, o_ready[j], back[1] + 1)
                    sp.dma_start(out_g[back[1] * RING + j], o_sb[:, j, :, :]).then_inc(stored[j], 16)

            run_slots(sp, slot, STORE_LAG, peeled=2)
            wait_all_stored(sp)

            sp.wait_ge(general_ready, 1)
            with sp.If(sp.value_load(general[0:1, 0:1]) != 0):
                for i, w in ((1, w_fwd), (2, w_bwd)):
                    sp.dma_start(w_nat[:, i, :], w).then_inc(g_weights_in, 16)
                for i, w in ((1, wg_fwd), (2, wg_bwd)):
                    sp.dma_start(wg_nat[:, i, :], w).then_inc(g_weights_in, 16)
                for i, (b, bg) in enumerate(((b_fwd, bg_fwd), (b_bwd, bg_bwd))):
                    sp.dma_start(rel_b[:, :, i, :], b.partition_broadcast(128)).then_inc(g_rel_in, 16)
                    sp.dma_start(rel_bg[:, :, i, :], bg.partition_broadcast(128)).then_inc(g_rel_in, 16)
                with sp.Fori(0, B) as b:
                    sp.dma_start(gx[:, :], x[b]).then_inc(g_in, 16)
                    sp.dma_start(gadj[:, :], adj[b]).then_inc(g_in, 16)
                    sp.wait_ge(g_o, b + 1)
                    sp.dma_start(out[b], go[:, :]).then_inc(g_stored, 16)
                    wait_apart(sp, g_stored, 16 * (b + 1))

        @block.gpsimd
        def _(pool):
            pool.memset(ident[:, :], 0.0).then_inc(ident_cleared, 1)
            pool.memset(ones[:, :], 1.0).then_inc(const_ready, 1)
            pool.memset(minus_half[:, :], -0.5).then_inc(const_ready, 1)
            pool.wait_ge(ident_cleared, 1)
            pool.affine_select(out=ident[:, :], in_=ident[:, :], compare_op=ALU.not_equal, fill=1.0,
                               base=0, pattern=[[-1, 128]], channel_multiplier=1).then_inc(ident_ready, 1)
            pool.wait_ge(const_ready, 2)

            def rstd_of(rnd, k):
                wait_apart(pool, stats_ready[k], rnd + 1)
                pool.tensor_scalar(var_eps[:, k, :], mean_var[:, k, :, 1], EPS, 1.0, ALU.add, ALU.mult)
                pool.tensor_scalar(neg_mean[:, k, :], mean_var[:, k, :, 0], -1.0, 0.0, ALU.mult, ALU.add)\
                    .then_inc(rstd_step, 1)
                step = 2 * (rnd * RING + k)
                pool.wait_ge(rstd_step, step + 1)
                pool.tensor_tensor(rstd[:, k, :], var_eps[:, k, :], minus_half[:, :], ALU.pow)\
                    .then_inc(rstd_step, 1)
                pool.wait_ge(rstd_step, step + 2)
                pool.tensor_tensor(shift[:, k, :], neg_mean[:, k, :], rstd[:, k, :], ALU.mult)\
                    .then_inc(shift_ready[k], 1)

            def slot(rnd, k):
                here = at(rnd, k, 0)
                if here is not None:
                    wait(pool, sums_done, at(rnd, k, RING))
                    wait_apart(pool, adj_in[k], 16 * (rnd + 1))
                    pool.tensor_scalar(mask[:, k, :, :], adj_sb[:, k, :, :], 1.0, 0.0, ALU.mult, ALU.add)\
                        .then_inc(mask_ready[k], 1)
                back = at(rnd, k, 3)
                if back is not None:
                    rstd_of(back[1], back[0])

            run_slots(pool, slot, 3)

            wait_all_stored(pool)
            pool.wait_ge(general_ready, 1)
            with pool.If(pool.value_load(general[0:1, 0:1]) != 0):
                pool.iota(rel_id[:, :], pattern=[[1, R]], base=FIRST_REL, channel_multiplier=0,
                          allow_small_or_imprecise_dtypes=True).then_inc(g_rel_id, 1)
                with pool.Fori(0, B) as b:
                    wait_apart(pool, g_in, 32 * (b + 1))
                    pool.tensor_copy(gadj_pair[:, 1, :], gadj[:, :]).then_inc(g_adj_f, 1)
                    wait_apart(pool, g_stat, 3 * b + 3)
                    pool.tensor_scalar(gve[:, :], gmv[:, 1:2], EPS, 1.0, ALU.add, ALU.mult).then_inc(g_rstd, 1)
                    pool.wait_ge(g_rstd, 2 * b + 1)
                    pool.tensor_tensor(grstd[:, :], gve[:, :], minus_half[:, 0:1], ALU.pow).then_inc(g_rstd, 1)

        @block.tensor
        def _(pe):
            pe.wait_ge(ident_ready, 1)
            pe.wait_ge(weights_in, 32)
            pe.transpose(xT_ps[0][:, 0:128], w_nat[:, 0, :], ident[:, :])
            pe.transpose(xT_ps[0][:, 128:256], wg_nat[:, 0, :], ident[:, :]).then_inc(wT_done, 1)
            pe.wait_ge(wT_copied, 1)
            pe.matmul(xT_ps[1][:, 0:128], w_nat[:, 0, :], wgT[:, 0, :], start=True, stop=True)\
                .then_inc(wprod_done, 1)

            def transpose_x(group, k):
                wait(pe, x_in, group, 16)
                for b in range(GB):
                    t = pe.transpose(xT_ps[k % 2][:, b * N:(b + 1) * N], x_sb[:, k, b, :], ident[:, :])
                t.then_inc(xT_done[k], 1)

            def project(group, k):
                hg = hg_ps[k % 2]
                for b in range(0, GB, 2):
                    pe.matmul(hg[:, b:b + 2, :, :], ones[:, :], bias_rows[:, :, :, :], start=True, stop=True)
                wait(pe, xT_ready, group)
                for b in range(GB):
                    mm = pe.matmul(hg[:, b, :, :], xT[:, k, b * N:(b + 1) * N], wcat_loop[:, :, :],
                                   start=False, stop=True, skip_group_check=True)
                mm.then_inc(hg_done[k], 1)

            def aggregate(group, k):
                wait(pe, mask_ready, group)
                wait(pe, vals_ready, group)
                for b in range(GB):
                    mm = pe.matmul(sum_ps[k % 2][:, b, :], mask[:, k, b, :], vals[:, k, b, :],
                                   start=True, stop=True)
                mm.then_inc(sums_done[k], 1)

            def slot(rnd, k):
                here = at(rnd, k, 0)
                if here is not None:
                    wait(pe, xT_ready, at(rnd, k, 2))
                    transpose_x(here, k)
                back = at(rnd, k, 1)
                if back is not None:
                    if isinstance(rnd, int) and rnd == 0 and k == 1:
                        pe.wait_ge(bias_step, 6)
                        pe.wait_ge(wcat_ready, 1)
                    wait(pe, vals_ready, at(rnd, k, 3))
                    project(back, back[0])
                back = at(rnd, k, 2)
                if back is not None:
                    wait(pe, y_ready, at(rnd, k, 4))
                    aggregate(back, back[0])

            pe.wait_ge(wcat_ready, 1)
            run_slots(pe, slot, 2)

            pe.wait_ge(row_max_ready, 1)
            pe.transpose(xT_ps[0][0:1, 0:128], row_max[:, 0:1], ident[:, :]).then_inc(row_max_T, 1)

            wait_all_stored(pe)
            pe.wait_ge(general_ready, 1)
            with pe.If(pe.value_load(general[0:1, 0:1]) != 0):
                pe.wait_ge(g_weights_in, 64)
                for i in (1, 2):
                    pe.transpose(xT_ps[0][:, (i - 1) * 128:i * 128], w_nat[:, i, :], ident[:, :])
                for i in (1, 2):
                    t = pe.transpose(xT_ps[0][:, (i + 1) * 128:(i + 2) * 128], wg_nat[:, i, :], ident[:, :])
                t.then_inc(g_wT_done, 1)
                pe.wait_ge(g_wT_copied, 1)
                for i in (1, 2):
                    mm = pe.matmul(xT_ps[1][:, (i - 1) * 128:i * 128], w_nat[:, i, :], wgT[:, i, :],
                                   start=True, stop=True)
                mm.then_inc(g_wprod_done, 1)
                pe.wait_ge(g_wcat_ready, 2)
                with pe.Fori(0, B) as b:
                    pe.wait_ge(g_adj_f, b + 1)
                    pe.transpose(xT_ps[0][:, 0:128], gx[:, :], ident[:, :])
                    pe.transpose(xT_ps[0][:, 128:256], gadj_pair[:, 1, :], ident[:, :]).then_inc(g_T_done, 1)
                    pe.wait_ge(g_T_ready, b + 1)
                    pe.matmul(xT_ps[1][:, :], gxT[:, :], wcat_dir[:, :, :], start=True, stop=True)
                    pe.matmul(hg_ps[0][:, 0:2, :, :], ones[:, :], bias_rows[:, :, :, :], start=True, stop=True)
                    pe.matmul(hg_ps[0][:, 0, :, :], gxT[:, :], wcat_loop[:, :, :], start=False, stop=True,
                              skip_group_check=True).then_inc(g_h_done, 1)
                    pe.wait_ge(g_loop_vals, b + 1)
                    pe.matmul(sum_ps[0][:, 0, :], gmask[:, 0, :], gvals[:, 0, :], start=True, stop=False,
                              skip_group_check=True).then_inc(g_loop_sum, 1)
                    with pe.Fori(0, R) as r:
                        pe.wait_ge(g_vals, b * R + r + 1)
                        for i in range(2):
                            mm = pe.matmul(sum_ps[0][:, 0, :], gmask[:, i, :], gvals[:, i, :], start=False,
                                           stop=False, skip_group_check=True)
                        mm.then_inc(g_rel_sum, 1)

        @block.scalar
        def _(act):
            def slot(rnd, k):
                here = at(rnd, k, 0)
                if here is not None:
                    wait(act, adj_in, here, 16)
                    group = rnd * RING + k
                    act.activation(excess[:, k, :, :], adj_sb[:, k, :, :].bitcast(U32), ACT.Relu, bias=-1.0,
                                   accum_out=row_excess[:, bass.ds(group, 1)]).then_inc(adj_tested[k], 1)
                    wait(act, xT_done, here)
                    wait(act, hg_done, at(rnd, k, RING))
                    act.activation(xT[:, k, :], xT_ps[k % 2][:, :], ACT.Copy).then_inc(xT_ready[k], 1)
                back = at(rnd, k, 1)
                if back is not None:
                    j = back[0]
                    wait(act, hg_done, back)
                    wait(act, vals_ready, at(rnd, k, 3))
                    act.activation(gate[:, j % 2, :, :], hg_ps[j % 2][:, :, 1, :], ACT.Sigmoid)\
                        .then_inc(gate_ready[j], 1)
                back = at(rnd, k, 4)
                if back is not None:
                    j = back[0]
                    wait(act, shift_ready, back)
                    wait(act, stored, at(rnd, k, 4 + RING), 16)
                    for b in range(GB):
                        a = act.activation(o_sb[:, j, b, :], y[:, j, b, :], ACT.Identity,
                                           bias=shift[:, j, b:b + 1], scale=rstd[:, j, b:b + 1])
                    a.then_inc(o_ready[j], 1)

            run_slots(act, slot, 4, peeled=2)

            wait_all_stored(act)
            act.wait_ge(general_ready, 1)
            with act.If(act.value_load(general[0:1, 0:1]) != 0):
                with act.Fori(0, B) as b:
                    act.wait_ge(g_h_done, b + 1)
                    act.activation(ggate[:, 0, :], hg_ps[0][:, 0, 1, :], ACT.Sigmoid).then_inc(g_loop_gate, 1)
                    with act.Fori(0, R) as r:
                        act.wait_ge(g_biased, b * R + r + 1)
                        act.activation(ggate[:, :, :], gg_b[:, :, :], ACT.Sigmoid).then_inc(g_gate, 1)

        @block.vector
        def _(dve):
            dve.wait_ge(bias_in, 32)
            dve.tensor_copy(bias_p[:, 0, :, :], bias_f[:, :, :]).then_inc(bias_step, 1)
            dve.wait_ge(bias_step, 1)
            dve.tensor_tensor(bias_r[:, :, :], bias_f[:, :, :], bias_p[:, 0, :, :], ALU.subtract)\
                .then_inc(bias_step, 1)
            dve.wait_ge(bias_step, 2)
            dve.tensor_copy(bias_p[:, 1, :, :], bias_r[:, :, :]).then_inc(bias_step, 1)
            dve.wait_ge(bias_step, 3)
            dve.tensor_tensor(bias_p[:, 2, :, :], bias_r[:, :, :], bias_p[:, 1, :, :], ALU.subtract)\
                .then_inc(bias_step, 1)
            dve.wait_ge(ident_ready, 1)
            dve.wait_ge(bias_step, 4)
            dve.tensor_scalar(bias_s[:, :, :], bias_p[:, 0, :, :], ident[:, 0:1], None, ALU.mult)\
                .then_inc(bias_step, 1)
            dve.wait_ge(bias_step, 5)
            dve.scalar_tensor_tensor(out=bias_r[:, :, :], in0=bias_p[:, 1, :, :], scalar=ident[:, 1:2],
                                     in1=bias_s[:, :, :], op0=ALU.mult, op1=ALU.add).then_inc(bias_step, 1)
            dve.wait_ge(bias_step, 6)
            for b in range(2):
                st = dve.scalar_tensor_tensor(out=bias_rows[:, b, :, :], in0=bias_p[:, 2, :, :],
                                              scalar=ident[:, 2:3], in1=bias_r[:, :, :], op0=ALU.mult,
                                              op1=ALU.add)
            st.then_inc(bias_step, 1)

            dve.wait_ge(wT_done, 1)
            dve.tensor_copy(wgT[:, 0, :], xT_ps[0][:, 128:256]).then_inc(wT_copied, 1)
            dve.tensor_copy(wcat_loop[:, 0, :], xT_ps[0][:, 0:128])
            dve.wait_ge(wprod_done, 1)
            dve.tensor_copy(wcat_loop[:, 1, :], xT_ps[1][:, 0:128]).then_inc(wcat_ready, 1)

            def slot(rnd, k):
                back = at(rnd, k, 1)
                if back is not None:
                    j = back[0]
                    wait(dve, gate_ready, back)
                    wait(dve, sums_done, at(rnd, k, 1 + RING))
                    dve.tensor_tensor(vals[:, j, :, :], hg_ps[j % 2][:, :, 0, :], gate[:, j % 2, :, :], ALU.mult)\
                        .then_inc(vals_ready[j], 1)
                back = at(rnd, k, 2)
                if back is not None:
                    j = back[0]
                    wait(dve, sums_done, back)
                    wait(dve, o_ready, at(rnd, k, 2 + RING))
                    dve.scalar_tensor_tensor(out=y[:, j, :, :], in0=sum_ps[j % 2][:, :, :], scalar=0.0,
                                             in1=x_sb[:, j, :, :], op0=ALU.max, op1=ALU.add)\
                        .then_inc(y_ready[j], 1)
                    wait(dve, y_ready, back)
                    for b in range(GB):
                        st = dve.bn_stats(bn[:, j, b, :], y[:, j, b, :])
                    st.then_inc(bn_done[j], 1)
                    wait_apart(dve, bn_done[j], back[1] + 1)
                    for b in range(GB):
                        st = dve.bn_aggr(mean_var[:, j, b, :], bn[:, j, b, :])
                    st.then_inc(stats_ready[j], 1)

            run_slots(dve, slot, 2, peeled=2)

            wait(dve, adj_tested, (RING - 1, ROUNDS - 1))
            dve.tensor_reduce(row_max[:, :], row_excess[:, :], AX.X, ALU.max).then_inc(row_max_ready, 1)
            dve.wait_ge(row_max_T, 1)
            dve.tensor_reduce(all_max[:, :], xT_ps[0][0:1, 0:128], AX.X, ALU.max).then_inc(all_max_ready, 1)
            dve.wait_ge(all_max_ready, 1)
            dve.tensor_scalar(general[:, :], all_max[:, :], 0.0, None, ALU.is_gt).then_inc(general_ready, 1)

            wait_all_stored(dve)
            dve.wait_ge(general_ready, 1)
            with dve.If(dve.value_load(general[0:1, 0:1]) != 0):
                dve.wait_ge(g_wT_done, 1)
                dve.tensor_copy(wgT[:, 1:3, :], xT_ps[0][:, 256:512].rearrange("p (a d) -> p a d", a=2))\
                    .then_inc(g_wT_copied, 1)
                dve.tensor_copy(wcat_dir[:, 0:2, :], xT_ps[0][:, 0:256].rearrange("p (a d) -> p a d", a=2))\
                    .then_inc(g_wcat_ready, 1)
                dve.wait_ge(g_wprod_done, 1)
                dve.tensor_copy(wcat_dir[:, 2:4, :], xT_ps[1][:, 0:256].rearrange("p (a d) -> p a d", a=2))\
                    .then_inc(g_wcat_ready, 1)
                dve.wait_ge(g_rel_in, 64)
                dve.wait_ge(g_rel_id, 1)
                with dve.Fori(0, B) as b:
                    dve.wait_ge(g_T_done, b + 1)
                    dve.tensor_copy(gxT[:, :], xT_ps[0][:, 0:128])
                    dve.tensor_copy(gadj_pair[:, 0, :], xT_ps[0][:, 128:256]).then_inc(g_T_ready, 1)
                    dve.wait_ge(g_h_done, b + 1)
                    dve.tensor_copy(gh[:, :, :], xT_ps[1][:, :].rearrange("p (a d) -> p a d", a=4))\
                        .then_inc(g_h_copied, 1)
                    dve.tensor_scalar(gmask[:, 0, :], gadj_pair[:, 1, :], 1.0, None, ALU.is_equal)
                    dve.wait_ge(g_loop_gate, b + 1)
                    dve.tensor_tensor(gvals[:, 0, :], hg_ps[0][:, 0, 0, :], ggate[:, 0, :], ALU.mult)\
                        .then_inc(g_loop_vals, 1)
                    dve.wait_ge(g_h_copied, b + 1)
                    dve.wait_ge(g_T_ready, b + 1)
                    wait_apart(dve, g_loop_sum, b + 1)
                    with dve.Fori(0, R) as r:
                        dve.tensor_tensor(gg_b[:, :, :], gh[:, 2:4, :], rel_bg[:, r, :, :], ALU.add)\
                            .then_inc(g_biased, 1)
                        dve.tensor_tensor(gh_b[:, :, :], gh[:, 0:2, :], rel_b[:, r, :, :], ALU.add)\
                            .then_inc(g_h_biased, 1)
                        dve.tensor_scalar(gmask[:, :, :], gadj_pair[:, :, :], rel_id[:, bass.ds(r, 1)], None,
                                          ALU.is_equal)
                        dve.wait_ge(g_gate, b * R + r + 1)
                        dve.wait_ge(g_h_biased, b * R + r + 1)
                        dve.tensor_tensor(gvals[:, :, :], gh_b[:, :, :], ggate[:, :, :], ALU.mult)\
                            .then_inc(g_vals, 1)
                        dve.wait_ge(g_rel_sum, b * R + r + 1)
                    dve.scalar_tensor_tensor(out=gy[:, :], in0=sum_ps[0][:, 0, :], scalar=0.0, in1=gx[:, :],
                                             op0=ALU.max, op1=ALU.add).then_inc(g_stat, 1)
                    dve.wait_ge(g_stat, 3 * b + 1)
                    dve.bn_stats(gbn[:, :], gy[:, :]).then_inc(g_stat, 1)
                    wait_apart(dve, g_stat, 3 * b + 2)
                    dve.bn_aggr(gmv[:, :], gbn[:, :]).then_inc(g_stat, 1)
                    dve.wait_ge(g_rstd, 2 * b + 2)
                    dve.tensor_scalar(go[:, :], gy[:, :], gmv[:, 0:1], grstd[:, 0:1], ALU.subtract, ALU.mult)\
                        .then_inc(g_o, 1)


_INS = ["x", "adj"] + [f"L0_gnn_{p}_{d}" for p in ("W", "Wg", "b", "bg") for d in ("fwd", "bwd", "loop")]


def kernel(**inputs):
    import concourse.bacc as bacc
    from concourse.bass_utils import run_bass_kernel_spmd

    nc = bacc.Bacc("TRN2", target_bir_lowering=False, num_devices=1)
    arrays, args = {}, []
    for name in _INS:
        a = np.ascontiguousarray(inputs[name])
        arrays[f"in_{name}"] = a
        args.append(nc.dram_tensor(f"in_{name}", a.shape, mybir.dt.from_np(a.dtype), kind="ExternalInput").ap())
    out = nc.dram_tensor("out", (B, N, D), F32, kind="ExternalOutput").ap()
    gnn_resnorm_kernel(nc, *args, out)
    result = run_bass_kernel_spmd(nc, [arrays], core_ids=[0])
    return result.results[0]["out"]
```

```python
from contextlib import ExitStack

import numpy as np

import concourse.bass as bass
from concourse import mybir

F32 = mybir.dt.float32
F32R = mybir.dt.float32r
BF16 = mybir.dt.bfloat16
I32 = mybir.dt.int32
U32 = mybir.dt.uint32
ALU = mybir.AluOpType
ACT = mybir.ActivationFunctionType
AX = mybir.AxisListType

B = 64
N = 128
D = 128
R = 39
FIRST_REL = 2
EPS = 1e-5
HALF = 64

GB = 4
GROUPS = B // GB
RING = 4
ROUNDS = GROUPS // RING
WARM_UP = 12
WARM_STEP = 3
ACT_NORM = 3
STORE_LAG = 7


def gnn_resnorm_kernel(nc, x, adj, w_fwd, w_bwd, w_loop, wg_fwd, wg_bwd, wg_loop,
                       b_fwd, b_bwd, b_loop, bg_fwd, bg_bwd, bg_loop, out):
    x_g = x.rearrange("(g b) n d -> g n b d", b=GB)
    adj_g = adj.rearrange("(g b) n m -> g n b m", b=GB)
    out_g = out.rearrange("(g b) n d -> g n b d", b=GB)

    ctx = ExitStack()
    with ctx:
        def sb(name, shape, dt):
            return ctx.enter_context(nc.sbuf_tensor(name, shape, dt))

        def sem(name):
            return ctx.enter_context(nc.semaphore(name))

        def ring_sem(name):
            return [sem(f"{name}{k}") for k in range(RING)]

        ident = sb("ident", [128, 128], F32)
        shares = sb("shares", [128, 128], F32R)
        minus_half = sb("minus_half", [128, GB], F32)
        w_nat = sb("w_nat", [128, 3, D], F32)
        wg_nat = sb("wg_nat", [128, 3, D], F32)
        wgT = sb("wgT", [128, 3, D], F32)
        wcat_hi = sb("wcat_hi", [128, 2, D], F32R)
        wcat_lo = sb("wcat_lo", [128, 2, D], F32R)
        bias_f = sb("bias_f", [128, 2, D], F32)
        bias_rows = sb("bias_rows", [128, 1, 2 * D], F32R)
        warm = sb("warm", [128, 1], F32)

        x_sb = sb("x_sb", [128, RING, GB, D], F32)
        adj_sb = sb("adj_sb", [128, RING, GB, N], I32)
        mask = sb("mask", [128, RING, GB, N], F32)
        xT_hi = sb("xT_hi", [128, RING, GB * N], F32R)
        xT_lo = sb("xT_lo", [128, RING, GB * N], F32R)
        gate = sb("gate", [128, 2, GB, D], F32)
        vals = sb("vals", [128, RING, GB, D], F32)
        y = sb("y", [128, RING, GB, D], F32)
        o_sb = sb("o_sb", [128, RING, GB, D], F32)
        stats = sb("stats", [128, RING, GB, 3], F32)
        var_eps = sb("var_eps", [128, RING, GB], F32)
        neg_mean = sb("neg_mean", [128, RING, GB], F32)
        rstd = sb("rstd", [128, RING, GB], F32)
        shift = sb("shift", [128, RING, GB], F32)

        excess = sb("excess", [128, RING, GB, N], BF16)
        row_excess = sb("row_excess", [128, GROUPS], F32)
        row_max = sb("row_max", [128, 1], F32)
        all_max = sb("all_max", [1, 1], F32)
        general = sb("general", [1, 1], I32)

        wcat = sb("wcat", [128, 2, 3, D], F32)
        rel_b = sb("rel_b", [128, R, 2, D], F32)
        rel_bg = sb("rel_bg", [128, R, 2, D], F32)
        rel_id = sb("rel_id", [128, R], F32)
        gx = sb("gx", [128, D], F32)
        gadj = sb("gadj", [128, N], I32)
        gadj_pair = sb("gadj_pair", [128, 2, N], F32)
        gxT = sb("gxT", [128, N], F32)
        gh = sb("gh", [128, 2, 3, D], F32)
        gh_b = sb("gh_b", [128, 2, D], F32)
        gg_b = sb("gg_b", [128, 2, D], F32)
        ggate = sb("ggate", [128, 2, D], F32)
        gvals = sb("gvals", [128, 2, D], F32)
        gmask = sb("gmask", [128, 2, N], F32)
        gy = sb("gy", [128, D], F32)
        gbn = sb("gbn", [128, 6], F32)
        gmv = sb("gmv", [128, 2], F32)
        gve = sb("gve", [128, 1], F32)
        grstd = sb("grstd", [128, 1], F32)
        go = sb("go", [128, D], F32)

        xT_ps = [ctx.enter_context(nc.psum_tensor(f"xT_ps{i}", [128, 512], F32)) for i in range(2)]
        hg_ps = [ctx.enter_context(nc.psum_tensor(f"hg_ps{i}", [128, GB, 2, D], F32)) for i in range(2)]
        sum_ps = [ctx.enter_context(nc.psum_tensor(f"sum_ps{i}", [128, GB, D], F32)) for i in range(2)]

        weights_in = sem("weights_in")
        bias_in = sem("bias_in")
        ident_cleared = sem("ident_cleared")
        ident_ready = sem("ident_ready")
        const_ready = sem("const_ready")
        wT_done = sem("wT_done")
        wT_copied = sem("wT_copied")
        wprod_done = sem("wprod_done")
        wcat_step = sem("wcat_step")
        bias_step = sem("bias_step")

        x_in = ring_sem("x_in")
        adj_in = ring_sem("adj_in")
        mask_ready = ring_sem("mask_ready")
        adj_tested = ring_sem("adj_tested")
        xT_done = ring_sem("xT_done")
        hi_ready = ring_sem("hi_ready")
        lo_ready = ring_sem("lo_ready")
        hg_done = ring_sem("hg_done")
        gate_ready = ring_sem("gate_ready")
        vals_ready = ring_sem("vals_ready")
        sums_done = ring_sem("sums_done")
        y_ready = ring_sem("y_ready")
        stats_ready = ring_sem("stats_ready")
        rstd_step = sem("rstd_step")
        shift_ready = ring_sem("shift_ready")
        o_ready_act = ring_sem("o_ready_act")
        o_ready_dve = ring_sem("o_ready_dve")
        stored = ring_sem("stored")

        waits_apart = sem("waits_apart")
        row_max_ready = sem("row_max_ready")
        row_max_T = sem("row_max_T")
        all_max_ready = sem("all_max_ready")
        general_ready = sem("general_ready")

        g_weights_in = sem("g_weights_in")
        g_rel_in = sem("g_rel_in")
        g_rel_id = sem("g_rel_id")
        g_wT_done = sem("g_wT_done")
        g_wT_copied = sem("g_wT_copied")
        g_wprod_done = sem("g_wprod_done")
        g_wcat_ready = sem("g_wcat_ready")
        g_in = sem("g_in")
        g_adj_f = sem("g_adj_f")
        g_T_done = sem("g_T_done")
        g_T_ready = sem("g_T_ready")
        g_h_done = sem("g_h_done")
        g_h_copied = sem("g_h_copied")
        g_loop_biased = sem("g_loop_biased")
        g_loop_h_biased = sem("g_loop_h_biased")
        g_loop_gate = sem("g_loop_gate")
        g_loop_vals = sem("g_loop_vals")
        g_loop_sum = sem("g_loop_sum")
        g_biased = sem("g_biased")
        g_h_biased = sem("g_h_biased")
        g_gate = sem("g_gate")
        g_vals = sem("g_vals")
        g_rel_sum = sem("g_rel_sum")
        g_stat = sem("g_stat")
        g_rstd = sem("g_rstd")
        g_o = sem("g_o")
        g_stored = sem("g_stored")

        def run_slots(eng, slot, lag, peeled=1):
            for s in range(peeled * RING):
                slot(s // RING, s % RING)
            with eng.Fori(peeled, ROUNDS) as rnd:
                for k in range(RING):
                    slot(rnd, k)
            for s in range(lag):
                slot(ROUNDS + s // RING, s % RING)

        def at(rnd, k, back):
            q = (k - back) // RING
            if isinstance(rnd, int) and not 0 <= rnd + q < ROUNDS:
                return None
            return (k - back) % RING, (rnd + q if q else rnd)

        def wait(eng, sems, group, unit=1):
            if group is not None:
                k, rnd = group
                eng.wait_ge(sems[k], (rnd + 1) * unit)

        def wait_apart(eng, one, value):
            eng.wait_ge(one, value)
            eng.sem_inc(waits_apart, 1)

        def act_norm(rnd, k):
            return GB // 2 if isinstance(rnd, int) and rnd == ROUNDS and k == RING - 1 else ACT_NORM

        def wait_all_stored(eng):
            for k in range(RING):
                eng.wait_ge(stored[k], 16 * ROUNDS)

        block = ctx.enter_context(nc.Block())

        @block.sync
        def _(sp):
            sp.dma_start(w_nat[:, 0, :], w_loop).then_inc(weights_in, 16)
            sp.dma_start(wg_nat[:, 0, :], wg_loop).then_inc(weights_in, 16)

            def slot(rnd, k):
                here = at(rnd, k, 0)
                if here is not None:
                    group = rnd * RING + k
                    if at(rnd, k, RING) is not None:
                        wait_apart(sp, adj_tested[k], rnd)
                        wait_apart(sp, mask_ready[k], rnd)
                        sp.dma_start(adj_sb[:, k, :, :], adj_g[group]).then_inc(adj_in[k], 16)
                        wait_apart(sp, y_ready[k], rnd)
                    sp.dma_start(x_sb[:, k, :, :], x_g[group]).then_inc(x_in[k], 16)
                    if at(rnd, k, RING) is None:
                        sp.dma_start(adj_sb[:, k, :, :], adj_g[group]).then_inc(adj_in[k], 16)
                back = at(rnd, k, STORE_LAG)
                if back is not None:
                    j = back[0]
                    wait_apart(sp, o_ready_act[j], back[1] + 1)
                    wait_apart(sp, o_ready_dve[j], back[1] + 1)
                    sp.dma_start(out_g[back[1] * RING + j], o_sb[:, j, :, :]).then_inc(stored[j], 16)

            run_slots(sp, slot, STORE_LAG, peeled=2)
            wait_all_stored(sp)

            sp.wait_ge(general_ready, 1)
            with sp.If(sp.value_load(general[0:1, 0:1]) != 0):
                for i, w in ((1, w_fwd), (2, w_bwd)):
                    sp.dma_start(w_nat[:, i, :], w).then_inc(g_weights_in, 16)
                for i, w in ((1, wg_fwd), (2, wg_bwd)):
                    sp.dma_start(wg_nat[:, i, :], w).then_inc(g_weights_in, 16)
                for i, (b, bg) in enumerate(((b_fwd, bg_fwd), (b_bwd, bg_bwd))):
                    sp.dma_start(rel_b[:, :, i, :], b.partition_broadcast(128)).then_inc(g_rel_in, 16)
                    sp.dma_start(rel_bg[:, :, i, :], bg.partition_broadcast(128)).then_inc(g_rel_in, 16)
                with sp.Fori(0, B) as b:
                    sp.dma_start(gx[:, :], x[b]).then_inc(g_in, 16)
                    sp.dma_start(gadj[:, :], adj[b]).then_inc(g_in, 16)
                    sp.wait_ge(g_o, b + 1)
                    sp.dma_start(out[b], go[:, :]).then_inc(g_stored, 16)
                    wait_apart(sp, g_stored, 16 * (b + 1))

        @block.gpsimd
        def _(pool):
            pool.memset(ident[:, :], 0.0).then_inc(ident_cleared, 1)
            pool.memset(shares[:, :].bitcast(F32), 1.0 / HALF).then_inc(const_ready, 1)
            pool.memset(minus_half[:, :], -0.5).then_inc(const_ready, 1)
            pool.wait_ge(ident_cleared, 1)
            pool.affine_select(out=ident[:, :], in_=ident[:, :], compare_op=ALU.not_equal, fill=1.0,
                               base=0, pattern=[[-1, 128]], channel_multiplier=1).then_inc(ident_ready, 1)
            pool.wait_ge(const_ready, 2)

            def rstd_of(rnd, k):
                wait_apart(pool, stats_ready[k], rnd + 1)
                pool.tensor_scalar(var_eps[:, k, :], stats[:, k, :, 2], 1.0 / D, EPS, ALU.mult, ALU.add)
                pool.tensor_scalar(neg_mean[:, k, :], stats[:, k, :, 1], -1.0, 0.0, ALU.mult, ALU.add)\
                    .then_inc(rstd_step, 1)
                step = 2 * (rnd * RING + k)
                pool.wait_ge(rstd_step, step + 1)
                pool.tensor_tensor(rstd[:, k, :], var_eps[:, k, :], minus_half[:, :], ALU.pow)\
                    .then_inc(rstd_step, 1)
                pool.wait_ge(rstd_step, step + 2)
                pool.tensor_tensor(shift[:, k, :], neg_mean[:, k, :], rstd[:, k, :], ALU.mult)\
                    .then_inc(shift_ready[k], 1)

            def slot(rnd, k):
                here = at(rnd, k, 0)
                if here is not None:
                    wait(pool, sums_done, at(rnd, k, RING))
                    wait_apart(pool, adj_in[k], 16 * (rnd + 1))
                    pool.tensor_scalar(mask[:, k, :, :], adj_sb[:, k, :, :], 1.0, 0.0, ALU.mult, ALU.add)\
                        .then_inc(mask_ready[k], 1)
                back = at(rnd, k, 3)
                if back is not None:
                    rstd_of(back[1], back[0])

            run_slots(pool, slot, 3)

            wait_all_stored(pool)
            pool.wait_ge(general_ready, 1)
            with pool.If(pool.value_load(general[0:1, 0:1]) != 0):
                pool.iota(rel_id[:, :], pattern=[[1, R]], base=FIRST_REL, channel_multiplier=0,
                          allow_small_or_imprecise_dtypes=True).then_inc(g_rel_id, 1)
                with pool.Fori(0, B) as b:
                    wait_apart(pool, g_in, 32 * (b + 1))
                    pool.tensor_copy(gadj_pair[:, 1, :], gadj[:, :]).then_inc(g_adj_f, 1)
                    wait_apart(pool, g_stat, 3 * b + 3)
                    pool.tensor_scalar(gve[:, :], gmv[:, 1:2], EPS, 1.0, ALU.add, ALU.mult).then_inc(g_rstd, 1)
                    pool.wait_ge(g_rstd, 2 * b + 1)
                    pool.tensor_tensor(grstd[:, :], gve[:, :], minus_half[:, 0:1], ALU.pow).then_inc(g_rstd, 1)

        @block.tensor
        def _(pe):
            def keep_busy(n):
                for _ in range(n):
                    pe.transpose(hg_ps[1][:, 0, 0, :], ident[:, :], ident[:, :])

            pe.wait_ge(ident_ready, 1)
            keep_busy(WARM_UP)
            pe.wait_ge(weights_in, 32)
            pe.transpose(sum_ps[0][:, 0, :], w_nat[:, 0, :], ident[:, :])
            pe.transpose(sum_ps[0][:, 1, :], wg_nat[:, 0, :], ident[:, :]).then_inc(wT_done, 1)
            keep_busy(WARM_STEP)
            pe.wait_ge(wT_copied, 1)
            pe.matmul(sum_ps[1][:, 0, :], w_nat[:, 0, :], wgT[:, 0, :], start=True, stop=True)\
                .then_inc(wprod_done, 1)
            keep_busy(WARM_STEP)

            def transpose_x(group, k):
                wait(pe, x_in, group, 16)
                for b in range(GB):
                    t = pe.transpose(xT_ps[k % 2][:, b * N:(b + 1) * N], x_sb[:, k, b, :], ident[:, :])
                t.then_inc(xT_done[k], 1)

            def start_with_bias(k):
                for b in range(0, GB, 2):
                    pe.matmul(hg_ps[k % 2][:, b:b + 2, :, :].rearrange("p b a d -> p b (a d)"), shares[:, :],
                              bias_rows[:, :, :].broadcast_to([128, 2, 2 * D]), start=True, stop=True)

            def project(k, graphs):
                for b in graphs:
                    for xT, w in ((xT_hi, wcat_hi), (xT_hi, wcat_lo), (xT_lo, wcat_hi)):
                        mm = pe.matmul(hg_ps[k % 2][:, b, :, :], xT[:, k, b * N:(b + 1) * N], w[:, :, :],
                                       start=False, stop=True, skip_group_check=True)
                return mm

            def aggregate(group, k):
                wait(pe, mask_ready, group)
                wait(pe, vals_ready, group)
                for b in range(GB):
                    mm = pe.matmul(sum_ps[k % 2][:, b, :], mask[:, k, b, :], vals[:, k, b, :],
                                   start=True, stop=True)
                mm.then_inc(sums_done[k], 1)

            def slot(rnd, k):
                here, projected, summed = at(rnd, k, 0), at(rnd, k, 1), at(rnd, k, 2)
                j = (k - 1) % RING
                early = isinstance(rnd, int) and rnd == 0 and k < 2

                def transpose_here():
                    if here is not None:
                        wait(pe, lo_ready, at(rnd, k, 2))
                        transpose_x(here, k)

                if early:
                    transpose_here()
                if projected is not None:
                    if early:
                        pe.wait_ge(bias_step, 2)
                        pe.wait_ge(wcat_step, 4)
                    wait(pe, vals_ready, at(rnd, k, 3))
                    start_with_bias(j)
                    wait(pe, lo_ready, projected)
                    project(j, range(0, 2))
                if not early:
                    transpose_here()
                if projected is not None:
                    project(j, range(2, 3))
                if summed is not None:
                    wait(pe, y_ready, at(rnd, k, 4))
                    aggregate(summed, summed[0])
                if projected is not None:
                    project(j, range(3, 4)).then_inc(hg_done[j], 1)

            run_slots(pe, slot, 2)

            pe.wait_ge(row_max_ready, 1)
            pe.transpose(xT_ps[0][0:1, 0:128], row_max[:, 0:1], ident[:, :]).then_inc(row_max_T, 1)

            wait_all_stored(pe)
            pe.wait_ge(general_ready, 1)
            with pe.If(pe.value_load(general[0:1, 0:1]) != 0):
                pe.wait_ge(g_weights_in, 64)
                for i in range(3):
                    pe.transpose(xT_ps[0][:, i * 128:(i + 1) * 128], w_nat[:, i, :], ident[:, :])
                for i in range(3):
                    t = pe.transpose(xT_ps[1][:, i * 128:(i + 1) * 128], wg_nat[:, i, :], ident[:, :])
                t.then_inc(g_wT_done, 1)
                pe.wait_ge(g_wT_copied, 1)
                for i in range(3):
                    mm = pe.matmul(sum_ps[0][:, i, :], w_nat[:, i, :], wgT[:, i, :], start=True, stop=True)
                mm.then_inc(g_wprod_done, 1)
                pe.wait_ge(g_wcat_ready, 2)
                with pe.Fori(0, B) as b:
                    pe.wait_ge(g_adj_f, b + 1)
                    pe.transpose(xT_ps[0][:, 0:128], gx[:, :], ident[:, :])
                    pe.transpose(xT_ps[0][:, 128:256], gadj_pair[:, 1, :], ident[:, :]).then_inc(g_T_done, 1)
                    pe.wait_ge(g_T_ready, b + 1)
                    for i in range(2):
                        mm = pe.matmul(hg_ps[i][:, 0:2, :, :].rearrange("p b a d -> p (b a d)")[:, 0:3 * D],
                                       gxT[:, :], wcat[:, i, :, :], start=True, stop=True)
                    mm.then_inc(g_h_done, 1)
                    pe.wait_ge(g_loop_vals, b + 1)
                    pe.matmul(sum_ps[0][:, 0, :], gmask[:, 0, :], gvals[:, 0, :], start=True, stop=False,
                              skip_group_check=True).then_inc(g_loop_sum, 1)
                    with pe.Fori(0, R) as r:
                        pe.wait_ge(g_vals, b * R + r + 1)
                        for i in range(2):
                            mm = pe.matmul(sum_ps[0][:, 0, :], gmask[:, i, :], gvals[:, i, :], start=False,
                                           stop=False, skip_group_check=True)
                        mm.then_inc(g_rel_sum, 1)

        @block.scalar
        def _(act):
            act.dma_start(bias_f[:, 0, :], b_loop.partition_broadcast(128)).then_inc(bias_in, 16)
            act.dma_start(bias_f[:, 1, :], bg_loop.partition_broadcast(128)).then_inc(bias_in, 16)
            act.wait_ge(ident_ready, 1)
            act.activation(warm[:, :], ident[:, 0:1], ACT.Sigmoid)

            def normalise(group, graphs):
                j = group[0]
                for b in graphs:
                    a = act.activation(o_sb[:, j, b, :], y[:, j, b, :], ACT.Identity,
                                       bias=shift[:, j, b:b + 1], scale=rstd[:, j, b:b + 1])
                return a

            def slot(rnd, k):
                here = at(rnd, k, 0)
                if here is not None:
                    wait(act, xT_done, here)
                    wait(act, hg_done, at(rnd, k, RING))
                    act.activation(xT_hi[:, k, :], xT_ps[k % 2][:, :], ACT.Copy).then_inc(hi_ready[k], 1)
                normalised = at(rnd, k, 4)
                if normalised is not None:
                    wait(act, shift_ready, normalised)
                    wait(act, stored, at(rnd, k, 4 + RING), 16)
                    normalise(normalised, range(act_norm(rnd, k) - 1))
                back = at(rnd, k, 1)
                if back is not None:
                    j = back[0]
                    wait(act, hg_done, back)
                    wait(act, vals_ready, at(rnd, k, 3))
                    act.activation(gate[:, j % 2, :, :], hg_ps[j % 2][:, :, 1, :], ACT.Sigmoid)\
                        .then_inc(gate_ready[j], 1)
                if normalised is not None:
                    last = act_norm(rnd, k) - 1
                    normalise(normalised, range(last, last + 1)).then_inc(o_ready_act[normalised[0]], 1)
                if here is not None:
                    wait(act, adj_in, here, 16)
                    group = rnd * RING + k
                    act.activation(excess[:, k, :, :], adj_sb[:, k, :, :].bitcast(U32), ACT.Relu, bias=-1.0,
                                   accum_out=row_excess[:, bass.ds(group, 1)]).then_inc(adj_tested[k], 1)

            run_slots(act, slot, 4, peeled=2)

            wait_all_stored(act)
            act.wait_ge(general_ready, 1)
            with act.If(act.value_load(general[0:1, 0:1]) != 0):
                with act.Fori(0, B) as b:
                    act.wait_ge(g_loop_biased, b + 1)
                    act.activation(ggate[:, 0, :], gg_b[:, 0, :], ACT.Sigmoid).then_inc(g_loop_gate, 1)
                    with act.Fori(0, R) as r:
                        act.wait_ge(g_biased, b * R + r + 1)
                        act.activation(ggate[:, :, :], gg_b[:, :, :], ACT.Sigmoid).then_inc(g_gate, 1)

        @block.vector
        def _(dve):
            dve.wait_ge(wT_done, 1)
            dve.tensor_copy(wgT[:, 0, :], sum_ps[0][:, 1, :]).then_inc(wT_copied, 1)

            def split_weights(part, ps, step):
                dve.tensor_copy(wcat_hi[:, part, :], ps).then_inc(wcat_step, 1)
                dve.wait_ge(wcat_step, step + 1)
                dve.tensor_tensor(wcat_lo[:, part, :], ps, wcat_hi[:, part, :].bitcast(F32), ALU.subtract)\
                    .then_inc(wcat_step, 1)

            split_weights(0, sum_ps[0][:, 0, :], 0)
            dve.wait_ge(bias_in, 32)
            dve.tensor_copy(bias_rows[:, 0, :], bias_f[:, :, :].rearrange("p a d -> p (a d)"))\
                .then_inc(bias_step, 1)
            dve.wait_ge(bias_step, 1)
            dve.tensor_tensor(bias_rows[HALF:128, 0, :], bias_f[HALF:128, :, :].rearrange("p a d -> p (a d)"),
                              bias_rows[HALF:128, 0, :].bitcast(F32), ALU.subtract).then_inc(bias_step, 1)
            dve.wait_ge(wprod_done, 1)
            split_weights(1, sum_ps[1][:, 0, :], 2)

            def slot(rnd, k):
                here = at(rnd, k, 0)
                if here is not None:
                    wait(dve, hg_done, at(rnd, k, RING))
                    wait(dve, hi_ready, here)
                    dve.tensor_tensor(xT_lo[:, k, :], xT_ps[k % 2][:, :], xT_hi[:, k, :].bitcast(F32), ALU.subtract)\
                        .then_inc(lo_ready[k], 1)
                summed = at(rnd, k, 2)
                if summed is not None:
                    j = summed[0]
                    wait(dve, sums_done, summed)
                    wait(dve, o_ready_act, at(rnd, k, 2 + RING))
                    wait(dve, o_ready_dve, at(rnd, k, 2 + RING))
                    dve.scalar_tensor_tensor(out=y[:, j, :, :], in0=sum_ps[j % 2][:, :, :], scalar=0.0,
                                             in1=x_sb[:, j, :, :], op0=ALU.max, op1=ALU.add)\
                        .then_inc(y_ready[j], 1)
                back = at(rnd, k, 1)
                if back is not None:
                    j = back[0]
                    wait(dve, gate_ready, back)
                    wait(dve, sums_done, at(rnd, k, 1 + RING))
                    dve.tensor_tensor(vals[:, j, :, :], hg_ps[j % 2][:, :, 0, :], gate[:, j % 2, :, :], ALU.mult)\
                        .then_inc(vals_ready[j], 1)
                if summed is not None:
                    j = summed[0]
                    wait(dve, y_ready, summed)
                    for b in range(0, GB, 2):
                        st = dve.bn_stats(stats[:, j, b:b + 2, :].rearrange("p b s -> p (b s)"),
                                          y[:, j, b:b + 2, :].rearrange("p b d -> p d b"))
                    st.then_inc(stats_ready[j], 1)
                back = at(rnd, k, 4)
                if back is not None:
                    j = back[0]
                    wait_apart(dve, shift_ready[j], back[1] + 1)
                    if at(rnd, k, 4 + RING) is not None:
                        wait_apart(dve, stored[j], 16 * back[1])
                    for b in range(act_norm(rnd, k), GB):
                        ts = dve.tensor_scalar(o_sb[:, j, b, :], y[:, j, b, :], rstd[:, j, b:b + 1],
                                               shift[:, j, b:b + 1], ALU.mult, ALU.add)
                    ts.then_inc(o_ready_dve[j], 1)

            run_slots(dve, slot, 4, peeled=2)

            wait(dve, adj_tested, (RING - 1, ROUNDS - 1))
            dve.tensor_reduce(row_max[:, :], row_excess[:, :], AX.X, ALU.max).then_inc(row_max_ready, 1)
            dve.wait_ge(row_max_T, 1)
            dve.tensor_reduce(all_max[:, :], xT_ps[0][0:1, 0:128], AX.X, ALU.max).then_inc(all_max_ready, 1)
            dve.wait_ge(all_max_ready, 1)
            dve.tensor_scalar(general[:, :], all_max[:, :], 0.0, None, ALU.is_gt).then_inc(general_ready, 1)

            wait_all_stored(dve)
            dve.wait_ge(general_ready, 1)
            with dve.If(dve.value_load(general[0:1, 0:1]) != 0):
                dve.wait_ge(g_wT_done, 1)
                dve.tensor_copy(wgT[:, :, :], xT_ps[1][:, 0:3 * D].rearrange("p (a d) -> p a d", a=3))\
                    .then_inc(g_wT_copied, 1)
                dve.tensor_copy(wcat[:, 0, :, :], xT_ps[0][:, 0:3 * D].rearrange("p (a d) -> p a d", a=3))\
                    .then_inc(g_wcat_ready, 1)
                dve.wait_ge(g_wprod_done, 1)
                dve.tensor_copy(wcat[:, 1, :, :], sum_ps[0][:, 0:3, :]).then_inc(g_wcat_ready, 1)
                dve.wait_ge(g_rel_in, 64)
                dve.wait_ge(g_rel_id, 1)
                with dve.Fori(0, B) as b:
                    dve.wait_ge(g_T_done, b + 1)
                    dve.tensor_copy(gxT[:, :], xT_ps[0][:, 0:128])
                    dve.tensor_copy(gadj_pair[:, 0, :], xT_ps[0][:, 128:256]).then_inc(g_T_ready, 1)
                    dve.wait_ge(g_h_done, b + 1)
                    for i in range(2):
                        cp = dve.tensor_copy(gh[:, i, :, :], hg_ps[i][:, 0:2, :, :]
                                             .rearrange("p b a d -> p (b a) d")[:, 0:3, :])
                    cp.then_inc(g_h_copied, 1)
                    dve.wait_ge(g_h_copied, b + 1)
                    dve.tensor_tensor(gg_b[:, 0, :], gh[:, 1, 0, :], bias_f[:, 1, :], ALU.add)\
                        .then_inc(g_loop_biased, 1)
                    dve.tensor_tensor(gh_b[:, 0, :], gh[:, 0, 0, :], bias_f[:, 0, :], ALU.add)\
                        .then_inc(g_loop_h_biased, 1)
                    dve.tensor_scalar(gmask[:, 0, :], gadj_pair[:, 1, :], 1.0, None, ALU.is_equal)
                    dve.wait_ge(g_loop_gate, b + 1)
                    dve.wait_ge(g_loop_h_biased, b + 1)
                    dve.tensor_tensor(gvals[:, 0, :], gh_b[:, 0, :], ggate[:, 0, :], ALU.mult)\
                        .then_inc(g_loop_vals, 1)
                    dve.wait_ge(g_T_ready, b + 1)
                    wait_apart(dve, g_loop_sum, b + 1)
                    with dve.Fori(0, R) as r:
                        dve.tensor_tensor(gg_b[:, :, :], gh[:, 1, 1:3, :], rel_bg[:, r, :, :], ALU.add)\
                            .then_inc(g_biased, 1)
                        dve.tensor_tensor(gh_b[:, :, :], gh[:, 0, 1:3, :], rel_b[:, r, :, :], ALU.add)\
                            .then_inc(g_h_biased, 1)
                        dve.tensor_scalar(gmask[:, :, :], gadj_pair[:, :, :], rel_id[:, bass.ds(r, 1)], None,
                                          ALU.is_equal)
                        dve.wait_ge(g_gate, b * R + r + 1)
                        dve.wait_ge(g_h_biased, b * R + r + 1)
                        dve.tensor_tensor(gvals[:, :, :], gh_b[:, :, :], ggate[:, :, :], ALU.mult)\
                            .then_inc(g_vals, 1)
                        dve.wait_ge(g_rel_sum, b * R + r + 1)
                    dve.scalar_tensor_tensor(out=gy[:, :], in0=sum_ps[0][:, 0, :], scalar=0.0, in1=gx[:, :],
                                             op0=ALU.max, op1=ALU.add).then_inc(g_stat, 1)
                    dve.wait_ge(g_stat, 3 * b + 1)
                    dve.bn_stats(gbn[:, :], gy[:, :]).then_inc(g_stat, 1)
                    wait_apart(dve, g_stat, 3 * b + 2)
                    dve.bn_aggr(gmv[:, :], gbn[:, :]).then_inc(g_stat, 1)
                    dve.wait_ge(g_rstd, 2 * b + 2)
                    dve.tensor_scalar(go[:, :], gy[:, :], gmv[:, 0:1], grstd[:, 0:1], ALU.subtract, ALU.mult)\
                        .then_inc(g_o, 1)


_INS = ["x", "adj"] + [f"L0_gnn_{p}_{d}" for p in ("W", "Wg", "b", "bg") for d in ("fwd", "bwd", "loop")]


def kernel(**inputs):
    import concourse.bacc as bacc
    from concourse.bass_utils import run_bass_kernel_spmd

    nc = bacc.Bacc("TRN2", target_bir_lowering=False, num_devices=1)
    arrays, args = {}, []
    for name in _INS:
        a = np.ascontiguousarray(inputs[name])
        arrays[f"in_{name}"] = a
        args.append(nc.dram_tensor(f"in_{name}", a.shape, mybir.dt.from_np(a.dtype), kind="ExternalInput").ap())
    out = nc.dram_tensor("out", (B, N, D), F32, kind="ExternalOutput").ap()
    gnn_resnorm_kernel(nc, *args, out)
    result = run_bass_kernel_spmd(nc, [arrays], core_ids=[0])
    return result.results[0]["out"]
```

```python
from contextlib import ExitStack

import numpy as np

import concourse.bass as bass
from concourse import mybir

F32 = mybir.dt.float32
F32R = mybir.dt.float32r
BF16 = mybir.dt.bfloat16
I32 = mybir.dt.int32
U32 = mybir.dt.uint32
ALU = mybir.AluOpType
ACT = mybir.ActivationFunctionType
AX = mybir.AxisListType

B = 64
N = 128
D = 128
R = 39
FIRST_REL = 2
EPS = 1e-5
HALF = 64

GB = 4
GROUPS = B // GB
RING = 4
ROUNDS = GROUPS // RING
WARM_UP = 12
WARM_STEP = 3
ACT_NORM = 3
ACT_NORM_END = (4, 4, 1, 0)
DVE_MOMENTS = 2
STORE_LAG = 7


def gnn_resnorm_kernel(nc, x, adj, w_fwd, w_bwd, w_loop, wg_fwd, wg_bwd, wg_loop,
                       b_fwd, b_bwd, b_loop, bg_fwd, bg_bwd, bg_loop, out):
    x_g = x.rearrange("(g b) n d -> g n b d", b=GB)
    adj_g = adj.rearrange("(g b) n m -> g n b m", b=GB)
    out_g = out.rearrange("(g b) n d -> g n b d", b=GB)

    ctx = ExitStack()
    with ctx:
        def sb(name, shape, dt):
            return ctx.enter_context(nc.sbuf_tensor(name, shape, dt))

        def sem(name):
            return ctx.enter_context(nc.semaphore(name))

        def ring_sem(name):
            return [sem(f"{name}{k}") for k in range(RING)]

        ident = sb("ident", [128, 128], F32)
        shares = sb("shares", [128, 128], F32R)
        minus_half = sb("minus_half", [128, GB], F32)
        w_nat = sb("w_nat", [128, 3, D], F32)
        wg_nat = sb("wg_nat", [128, 3, D], F32)
        wgT = sb("wgT", [128, 3, D], F32)
        wcat_hi = sb("wcat_hi", [128, 2, D], F32R)
        wcat_lo = sb("wcat_lo", [128, 2, D], F32R)
        bias_f = sb("bias_f", [128, 2, D], F32)
        bias_rows = sb("bias_rows", [128, 1, 2 * D], F32R)
        warm = sb("warm", [128, 1], F32)

        x_sb = sb("x_sb", [128, RING, GB, D], F32)
        adj_sb = sb("adj_sb", [128, RING, GB, N], I32)
        mask = sb("mask", [128, RING, GB, N], F32)
        xT_hi = sb("xT_hi", [128, RING, GB * N], F32R)
        xT_lo = sb("xT_lo", [128, RING, GB * N], F32R)
        gate = sb("gate", [128, 2, GB, D], F32)
        vals = sb("vals", [128, RING, GB, D], F32)
        y = sb("y", [128, RING, GB, D], F32)
        o_sb = sb("o_sb", [128, RING, GB, D], F32)
        stats = sb("stats", [128, RING, GB, 3], F32)
        var_eps = sb("var_eps", [128, RING, GB], F32)
        neg_mean = sb("neg_mean", [128, RING, GB], F32)
        rstd = sb("rstd", [128, RING, GB], F32)
        shift = sb("shift", [128, RING, GB], F32)

        excess = sb("excess", [128, RING, GB, N], BF16)
        row_excess = sb("row_excess", [128, GROUPS], F32)
        row_max = sb("row_max", [128, 1], F32)
        all_max = sb("all_max", [1, 1], F32)
        general = sb("general", [1, 1], I32)

        wcat = sb("wcat", [128, 2, 3, D], F32)
        rel_b = sb("rel_b", [128, R, 2, D], F32)
        rel_bg = sb("rel_bg", [128, R, 2, D], F32)
        rel_id = sb("rel_id", [128, R], F32)
        gx = sb("gx", [128, D], F32)
        gadj = sb("gadj", [128, N], I32)
        gadj_pair = sb("gadj_pair", [128, 2, N], F32)
        gxT = sb("gxT", [128, N], F32)
        gh = sb("gh", [128, 2, 3, D], F32)
        gh_b = sb("gh_b", [128, 2, D], F32)
        gg_b = sb("gg_b", [128, 2, D], F32)
        ggate = sb("ggate", [128, 2, D], F32)
        gvals = sb("gvals", [128, 2, D], F32)
        gmask = sb("gmask", [128, 2, N], F32)
        gy = sb("gy", [128, D], F32)
        gbn = sb("gbn", [128, 6], F32)
        gmv = sb("gmv", [128, 2], F32)
        gve = sb("gve", [128, 1], F32)
        grstd = sb("grstd", [128, 1], F32)
        go = sb("go", [128, D], F32)

        xT_ps = [ctx.enter_context(nc.psum_tensor(f"xT_ps{i}", [128, 512], F32)) for i in range(2)]
        hg_ps = [ctx.enter_context(nc.psum_tensor(f"hg_ps{i}", [128, GB, 2, D], F32)) for i in range(2)]
        sum_ps = [ctx.enter_context(nc.psum_tensor(f"sum_ps{i}", [128, GB, D], F32)) for i in range(2)]

        weights_in = sem("weights_in")
        bias_in = sem("bias_in")
        ident_cleared = sem("ident_cleared")
        ident_ready = sem("ident_ready")
        const_ready = sem("const_ready")
        wT_done = sem("wT_done")
        wT_copied = sem("wT_copied")
        wprod_done = sem("wprod_done")
        wcat_step = sem("wcat_step")
        bias_step = sem("bias_step")

        x_in = ring_sem("x_in")
        adj_in = ring_sem("adj_in")
        mask_ready = ring_sem("mask_ready")
        adj_tested = ring_sem("adj_tested")
        xT_done = ring_sem("xT_done")
        hi_ready = ring_sem("hi_ready")
        lo_ready = ring_sem("lo_ready")
        hg_done = ring_sem("hg_done")
        gate_ready = ring_sem("gate_ready")
        vals_ready = ring_sem("vals_ready")
        sums_done = ring_sem("sums_done")
        y_ready = ring_sem("y_ready")
        stats_ready = ring_sem("stats_ready")
        scaled = sem("scaled")
        moments_ready = sem("moments_ready")
        rstd_ready = sem("rstd_ready")
        shift_ready = ring_sem("shift_ready")
        o_ready_act = ring_sem("o_ready_act")
        o_ready_dve = ring_sem("o_ready_dve")
        stored = ring_sem("stored")
        half_projected = sem("half_projected")
        half_gated = sem("half_gated")
        half_valued = sem("half_valued")
        half_summed = sem("half_summed")
        half_y = sem("half_y")
        half_measured = sem("half_measured")
        half_normalised = sem("half_normalised")

        waits_apart = sem("waits_apart")
        row_max_ready = sem("row_max_ready")
        row_max_T = sem("row_max_T")
        all_max_ready = sem("all_max_ready")
        general_ready = sem("general_ready")

        g_weights_in = sem("g_weights_in")
        g_rel_in = sem("g_rel_in")
        g_rel_id = sem("g_rel_id")
        g_wT_done = sem("g_wT_done")
        g_wT_copied = sem("g_wT_copied")
        g_wprod_done = sem("g_wprod_done")
        g_wcat_ready = sem("g_wcat_ready")
        g_in = sem("g_in")
        g_adj_f = sem("g_adj_f")
        g_T_done = sem("g_T_done")
        g_T_ready = sem("g_T_ready")
        g_h_done = sem("g_h_done")
        g_h_copied = sem("g_h_copied")
        g_loop_biased = sem("g_loop_biased")
        g_loop_h_biased = sem("g_loop_h_biased")
        g_loop_gate = sem("g_loop_gate")
        g_loop_vals = sem("g_loop_vals")
        g_loop_sum = sem("g_loop_sum")
        g_biased = sem("g_biased")
        g_h_biased = sem("g_h_biased")
        g_gate = sem("g_gate")
        g_vals = sem("g_vals")
        g_rel_sum = sem("g_rel_sum")
        g_stat = sem("g_stat")
        g_rstd = sem("g_rstd")
        g_o = sem("g_o")
        g_stored = sem("g_stored")

        def run_slots(eng, slot, lag, peeled=1):
            for s in range(peeled * RING):
                slot(s // RING, s % RING)
            with eng.Fori(peeled, ROUNDS) as rnd:
                for k in range(RING):
                    slot(rnd, k)
            for s in range(lag):
                slot(ROUNDS + s // RING, s % RING)

        def at(rnd, k, back):
            q = (k - back) // RING
            if isinstance(rnd, int) and not 0 <= rnd + q < ROUNDS:
                return None
            return (k - back) % RING, (rnd + q if q else rnd)

        def wait(eng, sems, group, unit=1):
            if group is not None:
                k, rnd = group
                eng.wait_ge(sems[k], (rnd + 1) * unit)

        def wait_apart(eng, one, value):
            eng.wait_ge(one, value)
            eng.sem_inc(waits_apart, 1)

        def parts(group):
            last = isinstance(group[1], int) and group == (RING - 1, ROUNDS - 1)
            return (range(0, GB // 2), range(GB // 2, GB)) if last else (range(GB),)

        def span(graphs):
            return slice(graphs[0], graphs[-1] + 1)

        def wait_part(eng, sems, half, group, graphs):
            if graphs[-1] < GB - 1:
                eng.wait_ge(half, 1)
            else:
                wait(eng, sems, group)

        def part_sem(sems, half, group, graphs):
            return half if graphs[-1] < GB - 1 else sems[group[0]]

        def sums_of(group, graphs):
            if 0 < graphs[0] and len(parts(group)) > 1:
                return xT_ps[0][:, graphs[0] * D:(graphs[-1] + 1) * D].rearrange("p (b d) -> p b d", d=D)
            return sum_ps[group[0] % 2][:, span(graphs), :]

        def act_norm(group):
            k, rnd = group
            return ACT_NORM_END[k] if isinstance(rnd, int) and rnd == ROUNDS - 1 else ACT_NORM

        def moments_on_dve(group):
            k, rnd = group
            return isinstance(rnd, int) and rnd * RING + k >= GROUPS - DVE_MOMENTS

        def scale_var(eng, k, graphs):
            return eng.tensor_scalar(var_eps[:, k, span(graphs)], stats[:, k, span(graphs), 2], 1.0 / D, EPS,
                                     ALU.mult, ALU.add)

        def negate_mean(eng, k):
            return eng.tensor_scalar(neg_mean[:, k, :], stats[:, k, :, 1], -1.0, 0.0, ALU.mult, ALU.add)

        def wait_all_stored(eng):
            for k in range(RING - 1):
                eng.wait_ge(stored[k], 16 * ROUNDS)
            eng.wait_ge(stored[RING - 1], 16 * (ROUNDS + 1))

        block = ctx.enter_context(nc.Block())

        @block.sync
        def _(sp):
            sp.dma_start(w_nat[:, 0, :], w_loop).then_inc(weights_in, 16)
            sp.dma_start(wg_nat[:, 0, :], wg_loop).then_inc(weights_in, 16)

            def slot(rnd, k):
                here = at(rnd, k, 0)
                if here is not None:
                    group = rnd * RING + k
                    if at(rnd, k, RING) is not None:
                        wait_apart(sp, adj_tested[k], rnd)
                        wait_apart(sp, mask_ready[k], rnd)
                        sp.dma_start(adj_sb[:, k, :, :], adj_g[group]).then_inc(adj_in[k], 16)
                        wait_apart(sp, y_ready[k], rnd)
                    if at(rnd, k, 1) is not None:
                        sp.dma_start(x_sb[:, k, :, :], x_g[group]).then_inc(x_in[k], 16)
                    if at(rnd, k, RING) is None:
                        for j in {0: (), 1: (0, 1)}.get(k, (k,)):
                            sp.dma_start(adj_sb[:, j, :, :], adj_g[j]).then_inc(adj_in[j], 16)
                back = at(rnd, k, STORE_LAG)
                if back is not None:
                    j = back[0]
                    if act_norm(back) > 0:
                        wait_apart(sp, o_ready_act[j], back[1] + 1)
                    if act_norm(back) < GB:
                        wait_apart(sp, o_ready_dve[j], back[1] + 1)
                    graphs = span(parts(back)[-1])
                    sp.dma_start(out_g[back[1] * RING + j, :, graphs, :], o_sb[:, j, graphs, :])\
                        .then_inc(stored[j], 16)

            run_slots(sp, slot, STORE_LAG, peeled=2)
            wait_all_stored(sp)

            sp.wait_ge(general_ready, 1)
            with sp.If(sp.value_load(general[0:1, 0:1]) != 0):
                for i, w in ((1, w_fwd), (2, w_bwd)):
                    sp.dma_start(w_nat[:, i, :], w).then_inc(g_weights_in, 16)
                for i, w in ((1, wg_fwd), (2, wg_bwd)):
                    sp.dma_start(wg_nat[:, i, :], w).then_inc(g_weights_in, 16)
                for i, (b, bg) in enumerate(((b_fwd, bg_fwd), (b_bwd, bg_bwd))):
                    sp.dma_start(rel_b[:, :, i, :], b.partition_broadcast(128)).then_inc(g_rel_in, 16)
                    sp.dma_start(rel_bg[:, :, i, :], bg.partition_broadcast(128)).then_inc(g_rel_in, 16)
                with sp.Fori(0, B) as b:
                    sp.dma_start(gx[:, :], x[b]).then_inc(g_in, 16)
                    sp.dma_start(gadj[:, :], adj[b]).then_inc(g_in, 16)
                    sp.wait_ge(g_o, b + 1)
                    sp.dma_start(out[b], go[:, :]).then_inc(g_stored, 16)
                    wait_apart(sp, g_stored, 16 * (b + 1))

        @block.gpsimd
        def _(pool):
            pool.memset(ident[:, :], 0.0).then_inc(ident_cleared, 1)
            pool.memset(shares[:, :].bitcast(F32), 1.0 / HALF).then_inc(const_ready, 1)
            pool.memset(minus_half[:, :], -0.5).then_inc(const_ready, 1)
            pool.wait_ge(ident_cleared, 1)
            pool.affine_select(out=ident[:, :], in_=ident[:, :], compare_op=ALU.not_equal, fill=1.0,
                               base=0, pattern=[[-1, 128]], channel_multiplier=1).then_inc(ident_ready, 1)
            pool.wait_ge(bias_in, 32)
            pool.tensor_scalar(bias_rows[:, 0, :], bias_f[:, :, :].rearrange("p a d -> p (a d)"),
                               1.0, 0.0, ALU.mult, ALU.add).then_inc(bias_step, 1)
            pool.wait_ge(bias_step, 1)
            pool.tensor_tensor(bias_rows[HALF:128, 0, :], bias_f[HALF:128, :, :].rearrange("p a d -> p (a d)"),
                               bias_rows[HALF:128, 0, :].bitcast(F32), ALU.subtract).then_inc(bias_step, 1)
            pool.wait_ge(bias_step, 2)
            pool.wait_ge(const_ready, 2)

            def make_rstd(group):
                k, rnd = group
                count = rnd * RING + k + 1
                if not moments_on_dve(group):
                    wait_apart(pool, stats_ready[k], rnd + 1)
                    scale_var(pool, k, range(GB))
                    negate_mean(pool, k).then_inc(scaled, 1)
                    pool.wait_ge(scaled, count)
                for i, graphs in enumerate(parts(group)):
                    if moments_on_dve(group):
                        pool.wait_ge(moments_ready, DVE_MOMENTS - GROUPS + count + i)
                    pool.tensor_tensor(rstd[:, k, span(graphs)], var_eps[:, k, span(graphs)],
                                       minus_half[:, span(graphs)], ALU.pow).then_inc(rstd_ready, 1)
                if act_norm(group) > 0:
                    pool.wait_ge(rstd_ready, count)
                    pool.tensor_tensor(shift[:, k, :], neg_mean[:, k, :], rstd[:, k, :], ALU.mult)\
                        .then_inc(shift_ready[k], 1)

            def slot(rnd, k):
                here = at(rnd, k, 0)
                if here is not None:
                    wait(pool, sums_done, at(rnd, k, RING))
                    wait_apart(pool, adj_in[k], 16 * (rnd + 1))
                    pool.tensor_scalar(mask[:, k, :, :], adj_sb[:, k, :, :], 1.0, 0.0, ALU.mult, ALU.add)\
                        .then_inc(mask_ready[k], 1)
                back = at(rnd, k, 3)
                if back is not None:
                    make_rstd(back)

            run_slots(pool, slot, 3)

            wait_all_stored(pool)
            pool.wait_ge(general_ready, 1)
            with pool.If(pool.value_load(general[0:1, 0:1]) != 0):
                pool.iota(rel_id[:, :], pattern=[[1, R]], base=FIRST_REL, channel_multiplier=0,
                          allow_small_or_imprecise_dtypes=True).then_inc(g_rel_id, 1)
                with pool.Fori(0, B) as b:
                    wait_apart(pool, g_in, 32 * (b + 1))
                    pool.tensor_copy(gadj_pair[:, 1, :], gadj[:, :]).then_inc(g_adj_f, 1)
                    wait_apart(pool, g_stat, 3 * b + 3)
                    pool.tensor_scalar(gve[:, :], gmv[:, 1:2], EPS, 1.0, ALU.add, ALU.mult).then_inc(g_rstd, 1)
                    pool.wait_ge(g_rstd, 2 * b + 1)
                    pool.tensor_tensor(grstd[:, :], gve[:, :], minus_half[:, 0:1], ALU.pow).then_inc(g_rstd, 1)

        @block.tensor
        def _(pe):
            def keep_busy(n):
                for _ in range(n):
                    pe.transpose(hg_ps[1][:, 0, 0, :], ident[:, :], ident[:, :])

            def transpose_x(group, k):
                wait(pe, x_in, group, 16)
                for b in range(GB):
                    t = pe.transpose(xT_ps[k % 2][:, b * N:(b + 1) * N], x_sb[:, k, b, :], ident[:, :])
                t.then_inc(xT_done[k], 1)

            pe.wait_ge(ident_ready, 1)
            keep_busy(WARM_UP)
            pe.wait_ge(weights_in, 32)
            pe.transpose(sum_ps[0][:, 0, :], w_nat[:, 0, :], ident[:, :])
            pe.transpose(sum_ps[0][:, 1, :], wg_nat[:, 0, :], ident[:, :]).then_inc(wT_done, 1)
            transpose_x((0, 0), 0)
            pe.wait_ge(wT_copied, 1)
            pe.matmul(sum_ps[1][:, 0, :], w_nat[:, 0, :], wgT[:, 0, :], start=True, stop=True)\
                .then_inc(wprod_done, 1)
            def start_with_bias(k):
                for b in range(0, GB, 2):
                    pe.matmul(hg_ps[k % 2][:, b:b + 2, :, :].rearrange("p b a d -> p b (a d)"), shares[:, :],
                              bias_rows[:, :, :].broadcast_to([128, 2, 2 * D]), start=True, stop=True)

            def project_hi(k, graphs):
                for b in graphs:
                    for w in (wcat_hi, wcat_lo):
                        pe.matmul(hg_ps[k % 2][:, b, :, :], xT_hi[:, k, b * N:(b + 1) * N], w[:, :, :],
                                  start=False, stop=True, skip_group_check=True)

            def project_lo(k, graphs):
                for b in graphs:
                    mm = pe.matmul(hg_ps[k % 2][:, b, :, :], xT_lo[:, k, b * N:(b + 1) * N], wcat_hi[:, :, :],
                                   start=False, stop=True, skip_group_check=True)
                return mm

            def project(k, graphs):
                project_hi(k, graphs)
                return project_lo(k, graphs)

            def aggregate(group):
                k = group[0]
                wait(pe, mask_ready, group)
                for graphs in parts(group):
                    wait_part(pe, vals_ready, half_valued, group, graphs)
                    for b in graphs:
                        mm = pe.matmul(sums_of(group, graphs)[:, b - graphs[0], :], mask[:, k, b, :],
                                       vals[:, k, b, :], start=True, stop=True)
                    mm.then_inc(part_sem(sums_done, half_summed, group, graphs), 1)

            def slot(rnd, k):
                here, projected, summed = at(rnd, k, 0), at(rnd, k, 1), at(rnd, k, 2)
                j = (k - 1) % RING
                early = isinstance(rnd, int) and rnd == 0 and k < 2
                last = projected is not None and len(parts(projected)) > 1

                def transpose_here():
                    if here is not None:
                        wait(pe, lo_ready, at(rnd, k, 2))
                        transpose_x(here, k)

                if early and k:
                    transpose_here()
                if projected is not None:
                    if early:
                        pe.wait_ge(bias_step, 2)
                    wait(pe, vals_ready, at(rnd, k, 3))
                    start_with_bias(j)
                    if early:
                        pe.wait_ge(wcat_step, 4)
                    wait(pe, hi_ready, projected)
                    project_hi(j, range(0, 2))
                    wait(pe, lo_ready, projected)
                    mm = project_lo(j, range(0, 2))
                    if last:
                        mm.then_inc(half_projected, 1)
                        project(j, range(2, 4)).then_inc(hg_done[j], 1)
                if not early:
                    transpose_here()
                if projected is not None and not last:
                    project(j, range(2, 3))
                if summed is not None:
                    wait(pe, y_ready, at(rnd, k, 4))
                    aggregate(summed)
                if projected is not None and not last:
                    project(j, range(3, 4)).then_inc(hg_done[j], 1)

            run_slots(pe, slot, 2)

            pe.wait_ge(row_max_ready, 1)
            pe.transpose(xT_ps[0][0:1, 0:128], row_max[:, 0:1], ident[:, :]).then_inc(row_max_T, 1)

            wait_all_stored(pe)
            pe.wait_ge(general_ready, 1)
            with pe.If(pe.value_load(general[0:1, 0:1]) != 0):
                pe.wait_ge(g_weights_in, 64)
                for i in range(3):
                    pe.transpose(xT_ps[0][:, i * 128:(i + 1) * 128], w_nat[:, i, :], ident[:, :])
                for i in range(3):
                    t = pe.transpose(xT_ps[1][:, i * 128:(i + 1) * 128], wg_nat[:, i, :], ident[:, :])
                t.then_inc(g_wT_done, 1)
                pe.wait_ge(g_wT_copied, 1)
                for i in range(3):
                    mm = pe.matmul(sum_ps[0][:, i, :], w_nat[:, i, :], wgT[:, i, :], start=True, stop=True)
                mm.then_inc(g_wprod_done, 1)
                pe.wait_ge(g_wcat_ready, 2)
                with pe.Fori(0, B) as b:
                    pe.wait_ge(g_adj_f, b + 1)
                    pe.transpose(xT_ps[0][:, 0:128], gx[:, :], ident[:, :])
                    pe.transpose(xT_ps[0][:, 128:256], gadj_pair[:, 1, :], ident[:, :]).then_inc(g_T_done, 1)
                    pe.wait_ge(g_T_ready, b + 1)
                    for i in range(2):
                        mm = pe.matmul(hg_ps[i][:, 0:2, :, :].rearrange("p b a d -> p (b a d)")[:, 0:3 * D],
                                       gxT[:, :], wcat[:, i, :, :], start=True, stop=True)
                    mm.then_inc(g_h_done, 1)
                    pe.wait_ge(g_loop_vals, b + 1)
                    pe.matmul(sum_ps[0][:, 0, :], gmask[:, 0, :], gvals[:, 0, :], start=True, stop=False,
                              skip_group_check=True).then_inc(g_loop_sum, 1)
                    with pe.Fori(0, R) as r:
                        pe.wait_ge(g_vals, b * R + r + 1)
                        for i in range(2):
                            mm = pe.matmul(sum_ps[0][:, 0, :], gmask[:, i, :], gvals[:, i, :], start=False,
                                           stop=False, skip_group_check=True)
                        mm.then_inc(g_rel_sum, 1)

        @block.scalar
        def _(act):
            act.dma_start(x_sb[:, 0, :, :], x_g[0]).then_inc(x_in[0], 16)
            act.dma_start(bias_f[:, 0, :], b_loop.partition_broadcast(128)).then_inc(bias_in, 16)
            act.dma_start(bias_f[:, 1, :], bg_loop.partition_broadcast(128)).then_inc(bias_in, 16)
            act.wait_ge(ident_ready, 1)
            act.activation(warm[:, :], ident[:, 0:1], ACT.Sigmoid)

            def copy_hi(group):
                k, rnd = group
                wait(act, xT_done, group)
                wait(act, hg_done, at(rnd, k, RING))
                act.activation(xT_hi[:, k, :], xT_ps[k % 2][:, :], ACT.Copy).then_inc(hi_ready[k], 1)

            def make_gate(group):
                k, rnd = group
                wait(act, vals_ready, at(rnd, k, 2))
                for graphs in parts(group):
                    wait_part(act, hg_done, half_projected, group, graphs)
                    act.activation(gate[:, k % 2, span(graphs), :], hg_ps[k % 2][:, span(graphs), 1, :],
                                   ACT.Sigmoid).then_inc(part_sem(gate_ready, half_gated, group, graphs), 1)

            def normalise(group, graphs):
                k, rnd = group
                if graphs[0] == 0:
                    wait(act, shift_ready, group)
                    wait(act, stored, at(rnd, k, RING), 16)
                for b in graphs:
                    a = act.activation(o_sb[:, k, b, :], y[:, k, b, :], ACT.Identity,
                                       bias=shift[:, k, b:b + 1], scale=rstd[:, k, b:b + 1])
                if graphs[-1] == act_norm(group) - 1:
                    a.then_inc(o_ready_act[k], 1)

            def test(group):
                k, rnd = group
                wait(act, adj_in, group, 16)
                act.activation(excess[:, k, :, :], adj_sb[:, k, :, :].bitcast(U32), ACT.Relu, bias=-1.0,
                               accum_out=row_excess[:, bass.ds(rnd * RING + k, 1)]).then_inc(adj_tested[k], 1)

            def slot(rnd, k):
                here, gated, normalised = at(rnd, k, 0), at(rnd, k, 1), at(rnd, k, 4)
                copy_hi(here)
                if normalised is not None:
                    normalise(normalised, range(0, ACT_NORM - 1))
                if gated is not None:
                    make_gate(gated)
                if normalised is not None:
                    normalise(normalised, range(ACT_NORM - 1, ACT_NORM))
                test(here)

            run_slots(act, slot, 0, peeled=2)
            make_gate((RING - 1, ROUNDS - 1))
            for k in range(RING - 1):
                normalise((k, ROUNDS - 1), range(0, act_norm((k, ROUNDS - 1))))
            act.wait_ge(half_normalised, 1)
            act.dma_start(out_g[GROUPS - 1, :, 0:GB // 2, :], o_sb[:, RING - 1, 0:GB // 2, :])\
                .then_inc(stored[RING - 1], 16)

            wait_all_stored(act)
            act.wait_ge(general_ready, 1)
            with act.If(act.value_load(general[0:1, 0:1]) != 0):
                with act.Fori(0, B) as b:
                    act.wait_ge(g_loop_biased, b + 1)
                    act.activation(ggate[:, 0, :], gg_b[:, 0, :], ACT.Sigmoid).then_inc(g_loop_gate, 1)
                    with act.Fori(0, R) as r:
                        act.wait_ge(g_biased, b * R + r + 1)
                        act.activation(ggate[:, :, :], gg_b[:, :, :], ACT.Sigmoid).then_inc(g_gate, 1)

        @block.vector
        def _(dve):
            dve.wait_ge(wT_done, 1)
            dve.tensor_copy(wgT[:, 0, :], sum_ps[0][:, 1, :]).then_inc(wT_copied, 1)

            def split_weights(part, ps, step):
                dve.tensor_copy(wcat_hi[:, part, :], ps).then_inc(wcat_step, 1)
                dve.wait_ge(wcat_step, step + 1)
                dve.tensor_tensor(wcat_lo[:, part, :], ps, wcat_hi[:, part, :].bitcast(F32), ALU.subtract)\
                    .then_inc(wcat_step, 1)

            split_weights(0, sum_ps[0][:, 0, :], 0)
            dve.wait_ge(wprod_done, 1)
            split_weights(1, sum_ps[1][:, 0, :], 2)

            def copy_lo(group):
                k, rnd = group
                wait(dve, hg_done, at(rnd, k, RING))
                wait(dve, hi_ready, group)
                dve.tensor_tensor(xT_lo[:, k, :], xT_ps[k % 2][:, :], xT_hi[:, k, :].bitcast(F32), ALU.subtract)\
                    .then_inc(lo_ready[k], 1)

            def make_vals(group):
                k, rnd = group
                wait(dve, sums_done, at(rnd, k, RING))
                for graphs in parts(group):
                    wait_part(dve, gate_ready, half_gated, group, graphs)
                    dve.tensor_tensor(vals[:, k, span(graphs), :], hg_ps[k % 2][:, span(graphs), 0, :],
                                      gate[:, k % 2, span(graphs), :], ALU.mult)\
                        .then_inc(part_sem(vals_ready, half_valued, group, graphs), 1)

            def make_y(group, graphs):
                k, rnd = group
                wait(dve, o_ready_act, at(rnd, k, RING))
                wait(dve, o_ready_dve, at(rnd, k, RING))
                wait_part(dve, sums_done, half_summed, group, graphs)
                stt = dve.scalar_tensor_tensor(out=y[:, k, span(graphs), :], in0=sums_of(group, graphs),
                                               scalar=0.0, in1=x_sb[:, k, span(graphs), :], op0=ALU.max, op1=ALU.add)
                stt.then_inc(part_sem(y_ready, half_y, group, graphs), 1)

            def measure(group, graphs):
                k = group[0]
                wait_part(dve, y_ready, half_y, group, graphs)
                for b in graphs[::2]:
                    st = dve.bn_stats(stats[:, k, b:b + 2, :].rearrange("p b s -> p (b s)"),
                                      y[:, k, b:b + 2, :].rearrange("p b d -> p d b"))
                st.then_inc(part_sem(stats_ready, half_measured, group, graphs), 1)

            def normalise(group):
                k, rnd = group
                for i, graphs in enumerate(parts(group)):
                    wait_apart(dve, rstd_ready, rnd * RING + k + 1 + i)
                    if at(rnd, k, RING) is not None and i == 0:
                        wait_apart(dve, stored[k], 16 * rnd)
                    for b in graphs[act_norm(group):]:
                        ts = dve.tensor_scalar(o_sb[:, k, b, :], y[:, k, b, :], stats[:, k, b, 1:2],
                                               rstd[:, k, b:b + 1], ALU.subtract, ALU.mult)
                    ts.then_inc(part_sem(o_ready_dve, half_normalised, group, graphs), 1)

            def slot(rnd, k):
                gated, summed, normalised = at(rnd, k, 1), at(rnd, k, 2), at(rnd, k, 4)
                copy_lo(at(rnd, k, 0))
                if summed is not None:
                    make_y(summed, range(GB))
                if gated is not None:
                    make_vals(gated)
                if summed is not None:
                    measure(summed, range(GB))
                if normalised is not None:
                    normalise(normalised)

            run_slots(dve, slot, 0, peeled=2)
            before, last = (RING - 2, ROUNDS - 1), (RING - 1, ROUNDS - 1)
            first_half, second_half = parts(last)
            make_vals(last)
            make_y(before, range(GB))
            measure(before, range(GB))
            make_y(last, first_half)
            wait(dve, stats_ready, before)
            scale_var(dve, before[0], range(GB))
            negate_mean(dve, before[0]).then_inc(moments_ready, 1)
            make_y(last, second_half)
            measure(last, first_half)
            measure(last, second_half)
            for graphs in parts(last):
                wait_part(dve, stats_ready, half_measured, last, graphs)
                scale_var(dve, last[0], graphs).then_inc(moments_ready, 1)
            for k in range(RING):
                if act_norm((k, ROUNDS - 1)) < GB:
                    normalise((k, ROUNDS - 1))

            wait(dve, adj_tested, (RING - 1, ROUNDS - 1))
            dve.tensor_reduce(row_max[:, :], row_excess[:, :], AX.X, ALU.max).then_inc(row_max_ready, 1)
            dve.wait_ge(row_max_T, 1)
            dve.tensor_reduce(all_max[:, :], xT_ps[0][0:1, 0:128], AX.X, ALU.max).then_inc(all_max_ready, 1)
            dve.wait_ge(all_max_ready, 1)
            dve.tensor_scalar(general[:, :], all_max[:, :], 0.0, None, ALU.is_gt).then_inc(general_ready, 1)

            wait_all_stored(dve)
            dve.wait_ge(general_ready, 1)
            with dve.If(dve.value_load(general[0:1, 0:1]) != 0):
                dve.wait_ge(g_wT_done, 1)
                dve.tensor_copy(wgT[:, :, :], xT_ps[1][:, 0:3 * D].rearrange("p (a d) -> p a d", a=3))\
                    .then_inc(g_wT_copied, 1)
                dve.tensor_copy(wcat[:, 0, :, :], xT_ps[0][:, 0:3 * D].rearrange("p (a d) -> p a d", a=3))\
                    .then_inc(g_wcat_ready, 1)
                dve.wait_ge(g_wprod_done, 1)
                dve.tensor_copy(wcat[:, 1, :, :], sum_ps[0][:, 0:3, :]).then_inc(g_wcat_ready, 1)
                dve.wait_ge(g_rel_in, 64)
                dve.wait_ge(g_rel_id, 1)
                with dve.Fori(0, B) as b:
                    dve.wait_ge(g_T_done, b + 1)
                    dve.tensor_copy(gxT[:, :], xT_ps[0][:, 0:128])
                    dve.tensor_copy(gadj_pair[:, 0, :], xT_ps[0][:, 128:256]).then_inc(g_T_ready, 1)
                    dve.wait_ge(g_h_done, b + 1)
                    for i in range(2):
                        cp = dve.tensor_copy(gh[:, i, :, :], hg_ps[i][:, 0:2, :, :]
                                             .rearrange("p b a d -> p (b a) d")[:, 0:3, :])
                    cp.then_inc(g_h_copied, 1)
                    dve.wait_ge(g_h_copied, b + 1)
                    dve.tensor_tensor(gg_b[:, 0, :], gh[:, 1, 0, :], bias_f[:, 1, :], ALU.add)\
                        .then_inc(g_loop_biased, 1)
                    dve.tensor_tensor(gh_b[:, 0, :], gh[:, 0, 0, :], bias_f[:, 0, :], ALU.add)\
                        .then_inc(g_loop_h_biased, 1)
                    dve.tensor_scalar(gmask[:, 0, :], gadj_pair[:, 1, :], 1.0, None, ALU.is_equal)
                    dve.wait_ge(g_loop_gate, b + 1)
                    dve.wait_ge(g_loop_h_biased, b + 1)
                    dve.tensor_tensor(gvals[:, 0, :], gh_b[:, 0, :], ggate[:, 0, :], ALU.mult)\
                        .then_inc(g_loop_vals, 1)
                    dve.wait_ge(g_T_ready, b + 1)
                    wait_apart(dve, g_loop_sum, b + 1)
                    with dve.Fori(0, R) as r:
                        dve.tensor_tensor(gg_b[:, :, :], gh[:, 1, 1:3, :], rel_bg[:, r, :, :], ALU.add)\
                            .then_inc(g_biased, 1)
                        dve.tensor_tensor(gh_b[:, :, :], gh[:, 0, 1:3, :], rel_b[:, r, :, :], ALU.add)\
                            .then_inc(g_h_biased, 1)
                        dve.tensor_scalar(gmask[:, :, :], gadj_pair[:, :, :], rel_id[:, bass.ds(r, 1)], None,
                                          ALU.is_equal)
                        dve.wait_ge(g_gate, b * R + r + 1)
                        dve.wait_ge(g_h_biased, b * R + r + 1)
                        dve.tensor_tensor(gvals[:, :, :], gh_b[:, :, :], ggate[:, :, :], ALU.mult)\
                            .then_inc(g_vals, 1)
                        dve.wait_ge(g_rel_sum, b * R + r + 1)
                    dve.scalar_tensor_tensor(out=gy[:, :], in0=sum_ps[0][:, 0, :], scalar=0.0, in1=gx[:, :],
                                             op0=ALU.max, op1=ALU.add).then_inc(g_stat, 1)
                    dve.wait_ge(g_stat, 3 * b + 1)
                    dve.bn_stats(gbn[:, :], gy[:, :]).then_inc(g_stat, 1)
                    wait_apart(dve, g_stat, 3 * b + 2)
                    dve.bn_aggr(gmv[:, :], gbn[:, :]).then_inc(g_stat, 1)
                    dve.wait_ge(g_rstd, 2 * b + 2)
                    dve.tensor_scalar(go[:, :], gy[:, :], gmv[:, 0:1], grstd[:, 0:1], ALU.subtract, ALU.mult)\
                        .then_inc(g_o, 1)


_INS = ["x", "adj"] + [f"L0_gnn_{p}_{d}" for p in ("W", "Wg", "b", "bg") for d in ("fwd", "bwd", "loop")]


def kernel(**inputs):
    import concourse.bacc as bacc
    from concourse.bass_utils import run_bass_kernel_spmd

    nc = bacc.Bacc("TRN2", target_bir_lowering=False, num_devices=1)
    arrays, args = {}, []
    for name in _INS:
        a = np.ascontiguousarray(inputs[name])
        arrays[f"in_{name}"] = a
        args.append(nc.dram_tensor(f"in_{name}", a.shape, mybir.dt.from_np(a.dtype), kind="ExternalInput").ap())
    out = nc.dram_tensor("out", (B, N, D), F32, kind="ExternalOutput").ap()
    gnn_resnorm_kernel(nc, *args, out)
    result = run_bass_kernel_spmd(nc, [arrays], core_ids=[0])
    return result.results[0]["out"]
```
